# Optimizing a Trainium2 kernel written in Bass

```python
import numpy as np
import jax
import jax.numpy as jnp

def _softmax(x, axis=-1):
    return jax.nn.softmax(x, axis=axis)

def _gelu(x):
    return jax.nn.gelu(x, approximate=True)

def _silu(x):
    return jax.nn.silu(x)

def _sigmoid(x):
    return jax.nn.sigmoid(x)

def _layernorm(x, axis=-1, eps=1e-05):
    m = jnp.mean(x, axis=axis, keepdims=True)
    v = jnp.var(x, axis=axis, keepdims=True)
    return (x - m) / jnp.sqrt(v + eps)

def _scatter_add(tgt, idx, src, axis=0):
    return tgt.at[idx].add(src)

def _segment_sum(src, seg, n):
    return jax.ops.segment_sum(src, seg, n)
kernel_name = 'mk_audio_tower_d1_tok_audfeat512_r4_aff45f'

def setup_inputs(seed: int=0):
    np.random.seed(seed)
    _w = jnp.asarray

    def _rec_inputs():
        import jax
        import jax.numpy as jnp
        _rk = jax.random.key(seed)
        x = 3.78913e-05 + 1.00016 * jax.random.normal(jax.random.fold_in(_rk, 1), (32, 256, 64), jnp.float32)
        return x
    x = _rec_inputs()

    def _L0_tok_setup():
        import jax, jax.numpy as jnp
        import numpy as np
        CONTEXT = 5
        DILATION = 1
        EPS = 1e-05
        key = jax.random.key(seed)
        k1, k2, k3 = jax.random.split(key, 3)
        B, T, D, O = (64, 500, 64, 128)
        x = jax.random.normal(k1, (B, T, D), dtype=jnp.float32)
        K = D * CONTEXT
        W = jax.random.normal(k2, (O, K), dtype=jnp.float32) / np.sqrt(K).astype(np.float32)
        b = jax.random.normal(k3, (O,), dtype=jnp.float32) * 0.01
        gamma = jnp.ones((O,), dtype=jnp.float32)
        beta = jnp.zeros((O,), dtype=jnp.float32)
        return {'x': x, 'W': W, 'b': b, 'gamma': gamma, 'beta': beta}
    _L0_tok_all = _L0_tok_setup()
    _L0_tok_in = {k: v for k, v in _L0_tok_all.items() if k in ('W', 'b', 'gamma', 'beta')}
    del _L0_tok_all

    def _L0_attn_setup():
        import jax, jax.numpy as jnp
        import numpy as np
        NUM_HEADS = 16
        KERNEL_SIZE = 13
        key = jax.random.key(seed)
        ks = jax.random.split(key, 6)
        B, L, C = (4, 1024, 128)
        H, K = (NUM_HEADS, KERNEL_SIZE)
        x = jax.random.normal(ks[0], (B, L, C), dtype=jnp.float32)
        qkv_w = jax.random.normal(ks[1], (C, 3 * C), dtype=jnp.float32) * 0.02
        qkv_b = jnp.zeros((3 * C,), dtype=jnp.float32)
        rpb = jax.random.normal(ks[2], (H, 2 * K - 1), dtype=jnp.float32) * 0.02
        proj_w = jax.random.normal(ks[3], (C, C), dtype=jnp.float32) * 0.02
        proj_b = jnp.zeros((C,), dtype=jnp.float32)
        return {'x': x, 'qkv_w': qkv_w, 'qkv_b': qkv_b, 'rpb': rpb, 'proj_w': proj_w, 'proj_b': proj_b}
    _L0_attn_all = _L0_attn_setup()
    _L0_attn_in = {k: v for k, v in _L0_attn_all.items() if k in ('qkv_w', 'qkv_b', 'rpb', 'proj_w', 'proj_b')}
    del _L0_attn_all

    def _L0_ffn_setup():
        import jax, jax.numpy as jnp
        import numpy as np
        NUM_EXPERTS = 8
        TOP_K = 2
        HIDDEN = 128
        INTERMEDIATE = 512
        BATCH, SEQ = (8, 512)
        key = jax.random.key(seed)
        ks = jax.random.split(key, 7)
        s_in = 1.0 / np.sqrt(HIDDEN)
        s_mid = 1.0 / np.sqrt(INTERMEDIATE)
        return {'x': jax.random.normal(ks[0], (BATCH, SEQ, HIDDEN), jnp.float32), 'Wg': jax.random.normal(ks[1], (HIDDEN, NUM_EXPERTS), jnp.float32) * s_in, 'bg': jnp.zeros((NUM_EXPERTS,), jnp.float32), 'W1': jax.random.normal(ks[2], (NUM_EXPERTS, HIDDEN, INTERMEDIATE), jnp.float32) * s_in, 'b1': jnp.zeros((NUM_EXPERTS, INTERMEDIATE), jnp.float32), 'W2': jax.random.normal(ks[3], (NUM_EXPERTS, INTERMEDIATE, HIDDEN), jnp.float32) * s_mid, 'b2': jnp.zeros((NUM_EXPERTS, HIDDEN), jnp.float32)}
    _L0_ffn_all = _L0_ffn_setup()
    _L0_ffn_in = {k: v for k, v in _L0_ffn_all.items() if k in ('Wg', 'bg', 'W1', 'b1', 'W2', 'b2')}
    del _L0_ffn_all
    return {'x': x, 'L0_tok_W': _L0_tok_in['W'], 'L0_tok_b': _L0_tok_in['b'], 'L0_tok_gamma': _L0_tok_in['gamma'], 'L0_tok_beta': _L0_tok_in['beta'], 'L0_attn_qkv_w': _L0_attn_in['qkv_w'], 'L0_attn_qkv_b': _L0_attn_in['qkv_b'], 'L0_attn_rpb': _L0_attn_in['rpb'], 'L0_attn_proj_w': _L0_attn_in['proj_w'], 'L0_attn_proj_b': _L0_attn_in['proj_b'], 'L0_ffn_Wg': _L0_ffn_in['Wg'], 'L0_ffn_bg': _L0_ffn_in['bg'], 'L0_ffn_W1': _L0_ffn_in['W1'], 'L0_ffn_b1': _L0_ffn_in['b1'], 'L0_ffn_W2': _L0_ffn_in['W2'], 'L0_ffn_b2': _L0_ffn_in['b2']}

def reference(x, L0_tok_W, L0_tok_b, L0_tok_gamma, L0_tok_beta, L0_attn_qkv_w, L0_attn_qkv_b, L0_attn_rpb, L0_attn_proj_w, L0_attn_proj_b, L0_ffn_Wg, L0_ffn_bg, L0_ffn_W1, L0_ffn_b1, L0_ffn_W2, L0_ffn_b2):
    import jax
    import jax.numpy as jnp

    def _L0_tok_ref(x, W, b, gamma, beta):
        import jax, jax.numpy as jnp
        import numpy as np
        CONTEXT = 5
        DILATION = 1
        EPS = 1e-05
        B, T, D = x.shape
        new_T = T - DILATION * (CONTEXT - 1)
        win = jnp.concatenate([x[:, i * DILATION:i * DILATION + new_T, :] for i in range(CONTEXT)], axis=-1)
        y = jnp.einsum('btk,ok->bto', win, W) + b
        y = jax.nn.relu(y)
        mean = jnp.mean(y, axis=(0, 1))
        var = jnp.mean(jnp.square(y - mean), axis=(0, 1))
        y = (y - mean) * jax.lax.rsqrt(var + EPS) * gamma + beta
        return y

    def _L0_attn_ref(x, qkv_w, qkv_b, rpb, proj_w, proj_b):
        import jax, jax.numpy as jnp
        import numpy as np
        NUM_HEADS = 16
        KERNEL_SIZE = 13
        B, L, C = x.shape
        H, K = (NUM_HEADS, KERNEL_SIZE)
        hd = C // H
        scale = hd ** (-0.5)
        kh = K // 2
        qkv = (x @ qkv_w + qkv_b).reshape(B, L, 3, H, hd).transpose(2, 0, 3, 1, 4)
        q, k, v = (qkv[0] * scale, qkv[1], qkv[2])
        pos = jnp.arange(L)
        ni = jnp.clip(pos - kh, 0, L - K)
        idx = ni[:, None] + jnp.arange(K)[None, :]
        rpb_idx = (ni - pos + (K - 1))[:, None] + jnp.arange(K)[None, :]
        k_win = k[:, :, idx, :]
        v_win = v[:, :, idx, :]
        attn = jnp.einsum('bhld,bhlkd->bhlk', q, k_win) + rpb[:, rpb_idx][None]
        attn = jax.nn.softmax(attn, axis=-1)
        out = jnp.einsum('bhlk,bhlkd->bhld', attn, v_win)
        out = out.transpose(0, 2, 1, 3).reshape(B, L, C)
        return out @ proj_w + proj_b

    def _L0_ffn_ref(x, Wg, bg, W1, b1, W2, b2):
        import jax, jax.numpy as jnp
        import numpy as np
        NUM_EXPERTS = 8
        TOP_K = 2
        HIDDEN = 128
        INTERMEDIATE = 512
        BATCH, SEQ = (8, 512)
        B, S, H = x.shape
        xf = x.reshape(B * S, H)
        logits = xf @ Wg + bg
        probs = jax.nn.softmax(logits, axis=-1)
        _, top_idx = jax.lax.top_k(probs, TOP_K)
        mask = jnp.any(top_idx[:, :, None] == jnp.arange(NUM_EXPERTS)[None, None, :], axis=1)
        comb = probs * mask.astype(probs.dtype)
        out = jnp.zeros_like(xf)
        for e in range(NUM_EXPERTS):
            h = jax.nn.gelu(xf @ W1[e] + b1[e])
            y = h @ W2[e] + b2[e]
            out = out + comb[:, e:e + 1] * y
        return out.reshape(B, S, H)
    h = _L0_tok_ref(x, L0_tok_W, L0_tok_b, L0_tok_gamma, L0_tok_beta)
    h = h + _L0_attn_ref(_layernorm(h, axis=-1), L0_attn_qkv_w, L0_attn_qkv_b, L0_attn_rpb, L0_attn_proj_w, L0_attn_proj_b)
    h = h + _L0_ffn_ref(_layernorm(h, axis=-1), L0_ffn_Wg, L0_ffn_bg, L0_ffn_W1, L0_ffn_b1, L0_ffn_W2, L0_ffn_b2)
    return h

_drawn_inputs = setup_inputs


def setup_inputs(seed=0):
    import zlib

    import numpy as np

    out = dict(_drawn_inputs(seed))
    spreads = {'L0_tok_gamma': (1.0, 0.2),
     'L0_tok_beta': (0.0, 0.1),
     'L0_attn_qkv_b': (0.0, 0.1),
     'L0_attn_proj_b': (0.0, 0.1),
     'L0_ffn_bg': (0.0, 0.1),
     'L0_ffn_b1': (0.0, 0.294),
     'L0_ffn_b2': (0.0, 0.1)}
    factors = {'L0_tok_b': 4.67, 'L0_attn_rpb': 64.0}
    for name, (base, spread) in spreads.items():
        noise = np.random.default_rng([zlib.crc32(name.encode()), seed]).standard_normal(out[name].shape)
        drawn = base * np.exp(spread * noise) if base else spread * noise
        out[name] = jnp.asarray(drawn.astype(out[name].dtype))
    for name, factor in factors.items():
        out[name] = (out[name] * factor).astype(out[name].dtype)
    return out
```

```python
import concourse.bass as bass
from concourse import mybir
from concourse.alu_op_type import AluOpType as ALU
from contextlib import ExitStack

F32 = mybir.dt.float32
F16 = mybir.dt.float16
ACT = mybir.ActivationFunctionType
AX = mybir.AxisListType

B, S, D = 32, 256, 64
TAPS = 5
L = S - TAPS + 1
C = 128
NTOK = B * L
HEADS, HD = 16, 8
KS = 13
HALF = KS // 2
NE, FF = 8, 512
FC = FF // C
EPS = 1e-5
QSCALE = float(HD) ** -0.5

CB = 2
CT = CB * L
NC = B // CB
TT = 126
TPC = CT // TT
NT = NC * TPC
SUB = 63
NG = CT // SUB
JA = 8
JB = KS - JA
SPB = L // SUB
PSCALE = 16384.0

ROWS = {0: 0, SPB: 1, SPB - 1: 2, 2 * SPB - 1: 3}
for _g in range(NG):
    if _g not in ROWS:
        ROWS[_g] = len(ROWS)


def view(t, parts, offset, *dims, part0=0):
    row = 1
    for n in t.shape[1:]:
        row *= n
    return bass.AP(tensor=t[:].tensor, offset=offset + part0 * row, ap=[[row, parts], *[list(d) for d in dims]])


def tower(nc, x, tok_W, tok_b, tok_gamma, tok_beta, qkv_w, qkv_b, rpb, proj_w, proj_b,
          Wg, bg, W1, b1, W2, b2, out):
    ctx = ExitStack()
    with ctx:
        def sb(name, shape, dt=F32):
            return ctx.enter_context(nc.sbuf_tensor(name, shape, dt))

        def sem(name):
            return ctx.enter_context(nc.semaphore(name))

        ident = sb("ident", [128, 128])
        head_window = sb("head_window", [128, 240])
        head_expand = sb("head_expand", [128, NG, 128], F16)
        rel_bias = sb("rel_bias", [128, 2 * KS - 1])
        bias = sb("bias", [128, KS, SUB])
        w_nat = sb("w_nat", [C, TAPS * D])
        w_tap = sb("w_tap", [128, 3, C])
        qkv_sb = sb("qkv_sb", [C, 3 * C])
        proj_sb = sb("proj_sb", [C, C])
        wg_sb = sb("wg_sb", [C, NE])
        bg_sb = sb("bg_sb", [TT, NE])
        b1_sb = sb("b1_sb", [C, NE, FC])
        b2_sb = sb("b2_sb", [TT, NE, C])
        cols = sb("cols", [C, 8])
        tok_b_c, gamma_c, beta_c, proj_b_c = (cols[:, i:i + 1] for i in range(4))
        qkv_b_c = cols[:, 4:7]
        qb_c = cols[:, 7:8]

        chan = sb("chan", [C, NTOK])
        tokens = sb("tokens", [TT, NT, C])
        ln_stats = sb("ln_stats", [TT, NT, 6])
        ln_a = sb("ln_a", [TT, NT])
        ln_b = sb("ln_b", [TT, NT])
        ln_c = sb("ln_c", [TT, NT])
        rstd = sb("rstd", [TT, NT])
        nmr = sb("nmr", [TT, NT])
        bn_st = sb("bn_st", [C, NC, 6])
        bn_mv = sb("bn_mv", [C, 2])
        bn_w = sb("bn_w", [C, 4])

        xin = [sb(f"xin{i}", [128, 4, 2 * D]) for i in range(4)]
        xT = [sb(f"xT{i}", [128, CB * S]) for i in range(2)]
        xn = [sb(f"xn{i}", [TT, TPC, C]) for i in range(2)]
        xnT = [sb(f"xnT{i}", [C, CT]) for i in range(2)]
        zc = xnT
        q = [sb(f"q{i}", [C, CT]) for i in range(2)]
        k = [sb(f"k{i}", [C, CT]) for i in range(2)]
        v = [sb(f"v{i}", [C, CT]) for i in range(2)]
        qk = [sb(f"qk{i}", [C, KS, CT]) for i in range(2)]
        pv = chan
        ysum = sb("ysum", [TT, 2, FF])
        w1_sb = view(qk[0], C, FC * CT, [FF, NE], [1, FF])
        w2_sb = view(qk[1], C, FC * CT, [FF, NE], [C, FC], [1, C])
        sc = sb("sc", [128, KS, SUB])
        ex = sb("ex", [128, KS, SUB])
        mx = sb("mx", [128, SUB])
        sm = sb("sm", [128, SUB])
        rs = sb("rs", [128, SUB])
        p_hi = sb("p_hi", [128, KS, SUB], F16)
        p_lo = sb("p_lo", [128, KS, SUB], F16)
        oT = sb("oT", [C, CT])
        gate = sb("gate", [TT, NT, NE])
        gA = sb("gA", [TT, NT, NE])
        gB = sb("gB", [TT, NT, NE])
        gC = sb("gC", [TT, NT, NE])
        expert_rank = sb("expert_rank", [TT, NE])
        hid = qk

        bank = [ctx.enter_context(nc.psum_tensor(f"bank{i}", [128, 512], F32)) for i in range(8)]

        s_par = sem("s_par")
        s_w = sem("s_w")
        s_experts = sem("s_experts")
        s_const = sem("s_const")
        s_wT = sem("s_wT")
        s_wtap = sem("s_wtap")
        s_bias = sem("s_bias")
        s_xin = [sem(f"s_xin{i}") for i in range(4)]
        s_xtail = sem("s_xtail")
        s_xTp = sem("s_xTp")
        s_xT = sem("s_xT")
        s_conv = sem("s_conv")
        s_relu = sem("s_relu")
        s_bnst = sem("s_bnst")
        s_bn = sem("s_bn")
        s_bnsq = sem("s_bnsq")
        s_zc = sem("s_zc")
        s_zT = sem("s_zT")
        s_tok = sem("s_tok")
        s_lnst = sem("s_lnst")
        s_ln = sem("s_ln")
        s_lnsq = sem("s_lnsq")
        s_xn = sem("s_xn")
        s_xnTp = sem("s_xnTp")
        s_xnT = sem("s_xnT")
        s_qkvp = sem("s_qkvp")
        s_qkv = sem("s_qkv")
        s_qk = sem("s_qk")
        s_score = sem("s_score")
        s_sc = sem("s_sc")
        s_exp = sem("s_exp")
        s_hi = sem("s_hi")
        s_px = sem("s_px")
        s_pv = sem("s_pv")
        s_proj = sem("s_proj")
        s_oT = sem("s_oT")
        s_oback = sem("s_oback")
        s_res = sem("s_res")
        s_attn = sem("s_attn")
        s_g = sem("s_g")
        s_gexp = sem("s_gexp")
        s_gxn = sem("s_gxn")
        s_gT = sem("s_gT")
        s_gxT = sem("s_gxT")
        s_gall = sem("s_gall")
        s_lg = sem("s_lg")
        s_lgs = sem("s_lgs")
        s_h = sem("s_h")
        s_gelu = sem("s_gelu")
        s_y = sem("s_y")
        s_yb = sem("s_yb")
        s_acc = sem("s_acc")
        s_out = sem("s_out")

        block = ctx.enter_context(nc.Block())

        def wait(eng, semaphore, value):
            if isinstance(value, int) and value <= 0:
                return
            eng.wait_ge(semaphore, value)

        def valid(c):
            return not isinstance(c, int) or 0 <= c < NC

        def pairs(engine, body):
            body(0, 0)
            body(1, 1)
            with engine.Fori(1, NC // 2) as p:
                for par in range(2):
                    body(2 * p + par, par)

        def over_chunks(engine, body):
            def fixed(c):
                body(c, c % 2, lambda d: 0 <= c + d < NC)
            for c in range(-3, 2):
                fixed(c)
            with engine.Fori(1, (NC - 4) // 2) as p:
                for par in range(2):
                    body(2 * p + par, par, lambda d: True)
            for c in range(NC - 4, NC + 1):
                fixed(c)

        def tile_rows(t, c):
            return t[:, bass.ds(c * TPC, TPC), :]

        def chan_cols(c):
            return chan[:, bass.ds(c * CT, CT)]

        x_flat = x.rearrange("b s d -> (b s) d")
        out_flat = out.rearrange("b t c -> (b t) c")

        N_PAR = 9
        SMS = 7
        LN_STEPS = 7
        N_BIAS = NG

        @block.sync
        def _(sp):
            def load_x(c, buf, tiles=4):
                sp.dma_start(xin[buf][:, 0:tiles, :],
                             bass.AP(tensor=x.tensor, offset=c * CB * S * D, ap=[[D, 128], [128 * D, tiles], [1, 2 * D]])
                             ).then_inc(s_xin[buf], 16)

            sp.dma_start(w_nat[:, :], tok_W).then_inc(s_w, 16)
            for c in range(4):
                load_x(c, c)
            for i, vec in enumerate((tok_b, tok_gamma, tok_beta, proj_b)):
                sp.dma_start(cols[:, i:i + 1], vec.rearrange("(p a) -> p a", a=1)).then_inc(s_par, 16)
            sp.dma_start(qkv_b_c, qkv_b.rearrange("(a p) -> p a", p=C), allow_slow_non_contiguous=True).then_inc(s_par, 16)
            sp.dma_start(qkv_sb[:, :], qkv_w).then_inc(s_par, 16)
            sp.dma_start(proj_sb[:, :], proj_w).then_inc(s_par, 16)
            sp.dma_start(wg_sb[:, :], Wg).then_inc(s_par, 16)
            sp.dma_start(bg_sb[:, :], bg.partition_broadcast(TT)).then_inc(s_par, 16)
            for r in range(NG):
                sp.dma_start(rel_bias[16 * r:16 * r + 16, :], rpb).then_inc(s_bias, 16)
            with nc.sync.Fori(1, NC // 4 - 1) as p:
                for u in range(4):
                    c = 4 * p + u
                    sp.wait_ge(s_xTp, c - 3)
                    load_x(c, u)
            for u in range(4):
                c = NC - 4 + u
                sp.wait_ge(s_xTp, c - 3)
                if c == NC - 1:
                    row = B * S - 128
                    sp.dma_start(xin[u][0:127, 3, :], bass.AP(tensor=x.tensor, offset=row * D, ap=[[D, 127], [1, 2 * D]])
                                 ).then_inc(s_xtail, 16)
                    sp.dma_start(xin[u][127:128, 3, 0:D], x_flat[B * S - 1:B * S, :]).then_inc(s_xtail, 16)
                    sp.wait_ge(s_xtail, 32)
                load_x(c, u, 3 if c == NC - 1 else 4)
            sp.wait_ge(s_attn, NC)
            sp.dma_start(w1_sb[:, :, :], W1.rearrange("e c f -> c e f")).then_inc(s_experts, 16)
            sp.dma_start(w2_sb[:, :, :, :], W2.rearrange("e (i f) c -> f e i c", f=C)).then_inc(s_experts, 16)
            sp.dma_start(b1_sb[:, :, :], b1.rearrange("e (i f) -> f e i", f=C), allow_slow_non_contiguous=True).then_inc(s_experts, 16)
            sp.dma_start(b2_sb[:, :, :], b2.partition_broadcast(TT)).then_inc(s_experts, 16)
            with nc.sync.Fori(0, NC) as c:
                sp.wait_ge(s_acc, NE * c + NE)
                sp.dma_start(out_flat[bass.ds(c * CT, CT), :].rearrange("(k p) c -> p k c", p=TT),
                             tile_rows(tokens, c)).then_inc(s_out, 16)
            sp.wait_ge(s_out, 16 * NC)

        @block.gpsimd
        def _(pool):
            pool.memset(ident[:, :], 0.0).then_inc(s_const, 1)
            pool.memset(head_window[:, :], 0.0).then_inc(s_const, 1)
            pool.memset(head_expand[:, :, :], 0.0).then_inc(s_const, 1)
            pool.wait_ge(s_const, 3)
            pool.affine_select(out=ident[:, :], in_=ident[:, :], compare_op=ALU.not_equal, fill=1.0,
                               base=0, pattern=[[-1, 128]], channel_multiplier=1).then_inc(s_const, 1)
            pool.memset(head_window[:, 112:128], 1.0).then_inc(s_const, 1)
            pool.affine_select(out=head_expand[:, :, :], in_=head_expand[:, :, :], compare_op=ALU.not_equal,
                               fill=1.0, base=0, pattern=[[-16, NG], [-1, HEADS], [0, HD]],
                               channel_multiplier=1).then_inc(s_const, 1)
            pool.wait_ge(s_const, 6)
            pool.affine_select(out=head_window[:, 112:128], in_=head_window[:, 112:128], compare_op=ALU.is_ge,
                               fill=0.0, base=0, pattern=[[-HD, HEADS]], channel_multiplier=1).then_inc(s_const, 1)
            pool.wait_ge(s_const, 7)
            pool.affine_select(out=head_window[:, 112:128], in_=head_window[:, 112:128], compare_op=ALU.is_ge,
                               fill=0.0, base=HD - 1, pattern=[[HD, HEADS]], channel_multiplier=-1).then_inc(s_const, 1)
            pool.iota(expert_rank[:, :], pattern=[[-1, NE]], base=NE, channel_multiplier=0,
                      allow_small_or_imprecise_dtypes=True).then_inc(s_const, 1)
            def keep_input(c, par):
                pool.wait_ge(s_gxT, c + 1)
                nc.gpsimd.tensor_copy(chan_cols(c), xnT[par][:, :]).then_inc(s_gall, 1)

            pairs(nc.gpsimd, keep_input)

        @block.tensor
        def _(pe):
            pe.wait_ge(s_w, 16)
            pe.wait_ge(s_const, 4)
            nc.tensor.transpose(bank[7][:, 0:128], w_nat[:, 0:128], ident[:, :])
            nc.tensor.transpose(bank[7][:, 128:256], w_nat[:, 128:256], ident[:, :])
            nc.tensor.transpose(bank[7][0:64, 256:384], w_nat[:, 256:320], ident[:, :]).then_inc(s_wT, 1)
            pe.wait_ge(s_wtap, 1)

            def frames(c, buf, par):
                wait(pe, s_xT, c - 1)
                for t in range(4):
                    ins = nc.tensor.transpose(bank[par][:, 128 * t:128 * t + 128], xin[buf][:, t, :], ident[:, :])
                ins.then_inc(s_xTp, 1)

            def conv(c, par):
                pe.wait_ge(s_xT, c + 1)
                wait(pe, s_relu, c - 1)
                acc = bank[2 + par][:, 0:CT].rearrange("o (b t) -> o b t", b=CB)
                xv = xT[par][:, :].rearrange("p (b s) -> p b s", b=CB)
                nc.tensor.matmul(acc, w_tap[:, 0, :], xv[:, :, 0:L], start=True, stop=False)
                nc.tensor.matmul(acc, w_tap[:, 1, :], xv[:, :, 2:2 + L], start=False, stop=False)
                nc.tensor.matmul(acc, w_tap[0:64, 2, :], xv[0:64, :, 4:4 + L], start=False, stop=True
                                 ).then_inc(s_conv, 1)

            pe.wait_ge(s_xin[0], 16)
            frames(0, 0, 0)
            for c in range(1, 4):
                pe.wait_ge(s_xin[c], 16)
                frames(c, c, c % 2)
                conv(c - 1, (c - 1) % 2)
            with nc.tensor.Fori(1, NC // 4) as p:
                for u in range(4):
                    c = 4 * p + u
                    pe.wait_ge(s_xin[u], 16 * p + 16)
                    frames(c, u, u % 2)
                    conv(c - 1, (u - 1) % 2)
            conv(NC - 1, (NC - 1) % 2)

            def tiles(c, par):
                pe.wait_ge(s_zc, c + 1)
                wait(pe, s_tok, c - 1)
                for t in range(TPC):
                    ins = nc.tensor.transpose(bank[par][0:TT, C * t:C * t + C],
                                              zc[par][:, TT * t:TT * t + TT], ident[:, :])
                ins.then_inc(s_zT, 1)

            pairs(nc.tensor, tiles)

            def transposes(c, par):
                pe.wait_ge(s_xn, c + 1)
                wait(pe, s_res, c - 3)
                for t in range(TPC):
                    ins = nc.tensor.transpose(bank[0][:, TT * t:TT * t + TT], xn[par][:, t, :], ident[0:TT, 0:TT])
                ins.then_inc(s_xnTp, 1)

            def qkv(c, par):
                pe.wait_ge(s_xnT, c + 1)
                wait(pe, s_oT, c - 2)
                for i, b in enumerate((1, 0, 1)):
                    if i == 2:
                        pe.wait_ge(s_qkv, 3 * c + 1)
                    nc.tensor.matmul(bank[b][:, 0:CT], qkv_sb[:, C * i:C * i + C], xnT[par][:, :],
                                     start=True, stop=True).then_inc(s_qkvp, 1)

            def scores(c, par):
                pe.wait_ge(s_qk, c + 1)
                wait(pe, s_sc, SMS * (c - 1) + 1)
                for j0, nj, b in ((0, JA, 2), (JA, JB, 3)):
                    for g in range(NG):
                        col = 112 - 16 * ROWS[g]
                        ins = nc.tensor.matmul(bank[b][:, 0:nj * SUB].rearrange("p (j n) -> p j n", j=nj),
                                               head_window[:, col:col + 128],
                                               qk[par][:, j0:j0 + nj, SUB * g:SUB * g + SUB],
                                               start=(g == 0), stop=(g == NG - 1))
                ins.then_inc(s_score, 1)

            def spread(c):
                pe.wait_ge(s_hi, c + 1)
                pe.wait_ge(s_sc, SMS * c + SMS)
                for g in range(NG):
                    wait(pe, s_pv, NG * c + g - 1)
                    for j0, nj, b in ((0, JA, 4), (JA, JB, 5)):
                        dst = bank[b + 2 * (g % 2)][:, 0:nj * SUB]
                        lhsT = head_expand[:, ROWS[g], :]
                        nc.tensor.matmul(dst, lhsT, p_hi[:, j0:j0 + nj, :].rearrange("p j n -> p (j n)"),
                                         start=True, stop=False)
                        ins = nc.tensor.matmul(dst, lhsT, p_lo[:, j0:j0 + nj, :].rearrange("p j n -> p (j n)"),
                                               start=False, stop=True)
                    ins.then_inc(s_px, 1)

            def project(c):
                pe.wait_ge(s_pv, NG * c + NG)
                if valid(c + 2):
                    pe.wait_ge(s_qkv, 3 * (c + 2) + 3)
                wait(pe, s_oT, c)
                for j in range(KS):
                    ins = nc.tensor.matmul(bank[1][:, 0:CT], proj_sb[:, :], pv[:, CT * j:CT * j + CT],
                                           start=(j == 0), stop=(j == KS - 1))
                ins.then_inc(s_proj, 1)

            def back(c):
                pe.wait_ge(s_oT, c + 1)
                if valid(c + 3):
                    pe.wait_ge(s_qkv, 3 * (c + 3) + 2)
                else:
                    wait(pe, s_res, c)
                for t in range(TPC):
                    ins = nc.tensor.transpose(bank[0][0:TT, C * t:C * t + C], oT[:, TT * t:TT * t + TT], ident[:, :])
                ins.then_inc(s_oback, 1)

            def attention(c, par, inside):
                if inside(2):
                    transposes(c + 2, par)
                if inside(0):
                    spread(c)
                if inside(2):
                    qkv(c + 2, par)
                if inside(-1):
                    back(c - 1)
                if inside(1):
                    scores(c + 1, 1 - par)
                if inside(0):
                    project(c)

            pe.wait_ge(s_const, 8)
            over_chunks(nc.tensor, attention)

            def gate_logits(c, par):
                pe.wait_ge(s_gxn, c + 1)
                wait(pe, s_gxT, c - 1)
                for t in range(TPC):
                    ins = nc.tensor.transpose(bank[par][:, TT * t:TT * t + TT], xn[par][:, t, :],
                                              ident[0:TT, 0:TT])
                ins.then_inc(s_gT, 1)
                pe.wait_ge(s_gxT, c + 1)
                wait(pe, s_lgs, c - 1)
                for t in range(TPC):
                    ins = nc.tensor.matmul(bank[2 + par][0:TT, NE * t:NE * t + NE],
                                           xnT[par][:, TT * t:TT * t + TT], wg_sb[:, :], start=True, stop=True)
                ins.then_inc(s_lg, 1)

            pairs(nc.tensor, gate_logits)

            pe.wait_ge(s_experts, 64)
            pe.wait_ge(s_gall, NC)
            pe.wait_ge(s_lgs, NC)

            def hidden(c, e):
                for i in range(FC):
                    wait(pe, s_gelu, FC * (NE * c + e - 1) + i + 1)
                    nc.tensor.matmul(bank[i][:, 0:CT], view(qk[0], C, FC * CT + FF * e + C * i, [1, C]), chan_cols(c),
                                     start=True, stop=True).then_inc(s_h, 1)

            def outer(c, e):
                pe.wait_ge(s_gelu, FC * (NE * c + e + 1))
                wait(pe, s_yb, NE * c + e - 1)
                for t in range(TPC):
                    for i in range(FC):
                        ins = nc.tensor.matmul(bank[4 + e % 2][0:TT, C * t:C * t + C],
                                               hid[e % 2][:, i, TT * t:TT * t + TT], view(qk[1], C, FC * CT + FF * e + C * i, [1, C]),
                                               start=(i == 0), stop=(i == FC - 1))
                ins.then_inc(s_y, 1)

            def experts(c):
                hidden(c, 0)
                for e in range(1, NE):
                    hidden(c, e)
                    outer(c, e - 1)
                outer(c, NE - 1)

            experts(0)
            with nc.tensor.Fori(1, NC) as c:
                experts(c)

        @block.scalar
        def _(act):
            act.wait_ge(s_wT, 1)
            nc.scalar.copy(w_tap[:, 0:2, :].rearrange("p a o -> p (a o)"), bank[7][:, 0:256])
            nc.scalar.copy(w_tap[0:64, 2, :], bank[7][0:64, 256:384]).then_inc(s_wtap, 1)

            def keep_frames(c, par):
                act.wait_ge(s_xTp, c + 1)
                wait(act, s_conv, c - 1)
                nc.scalar.copy(xT[par][:, :], bank[par][:, :]).then_inc(s_xT, 1)

            def relu(c, par):
                act.wait_ge(s_conv, c + 1)
                nc.scalar.activation(chan_cols(c), bank[2 + par][:, 0:CT], ACT.Relu, bias=tok_b_c
                                     ).then_inc(s_relu, 1)

            act.wait_ge(s_par, 16 * N_PAR)
            keep_frames(0, 0)
            for c in range(1, 4):
                keep_frames(c, c % 2)
                relu(c - 1, (c - 1) % 2)
            with nc.scalar.Fori(1, NC // 4) as p:
                for u in range(4):
                    c = 4 * p + u
                    keep_frames(c, u % 2)
                    relu(c - 1, (u - 1) % 2)
            relu(NC - 1, (NC - 1) % 2)

            act.wait_ge(s_bn, 2)
            nc.scalar.activation(bn_w[:, 1:2], bn_w[:, 0:1], ACT.Sqrt).then_inc(s_bnsq, 1)

            def keep_tiles(c, par):
                act.wait_ge(s_zT, c + 1)
                nc.scalar.copy(tile_rows(tokens, c), bank[par][0:TT, :].rearrange("p (t c) -> p t c", t=TPC)
                               ).then_inc(s_tok, 1)

            pairs(nc.scalar, keep_tiles)

            act.wait_ge(s_ln, LN_STEPS)
            nc.scalar.activation(ln_c[:, :], ln_b[:, :], ACT.Sqrt).then_inc(s_lnsq, 1)

            def normalise(c, par, signal):
                for t in range(TPC):
                    i = c * TPC + t
                    ins = nc.scalar.activation(xn[par][:, t, :], view_tile(i), ACT.Identity,
                                               bias=nmr[:, bass.ds(i, 1)], scale=rstd[:, bass.ds(i, 1)])
                ins.then_inc(signal, 1)

            def view_tile(i):
                return tokens[:, bass.ds(i, 1), :].rearrange("p a c -> p (a c)")

            def attention(c, par, inside):
                if inside(-1):
                    act.wait_ge(s_proj, c)
                    wait(act, s_oback, c - 1)
                    nc.scalar.activation(oT[:, :], bank[1][:, 0:CT], ACT.Identity, bias=proj_b_c,
                                         scale=1.0 / PSCALE).then_inc(s_oT, 1)
                if inside(2):
                    act.wait_ge(s_xnTp, c + 3)
                    wait(act, s_qkvp, 3 * (c + 1))
                    nc.scalar.copy(xnT[par][:, :], bank[0][:, 0:CT]).then_inc(s_xnT, 1)
                    for i, (dst, b) in enumerate(((q, 1), (k, 0), (v, 1))):
                        act.wait_ge(s_qkvp, 3 * (c + 2) + i + 1)
                        if i == 0:
                            wait(act, s_qk, c + 1)
                        if i == 2:
                            wait(act, s_pv, NG * (c + 1))
                        nc.scalar.activation(dst[par][:, :], bank[b][:, 0:CT], ACT.Identity,
                                             bias=qb_c if i == 0 else qkv_b_c[:, i:i + 1],
                                             scale=QSCALE if i == 0 else 1.0).then_inc(s_qkv, 1)
                if inside(3):
                    wait(act, s_xnTp, c + 2)
                    normalise(c + 3, 1 - par, s_xn)
                if inside(1):
                    act.wait_ge(s_sc, SMS * (c + 1) + 3)
                    nc.scalar.activation(ex[:, :, :], sc[:, :, :], ACT.Exp).then_inc(s_exp, 1)
                    act.wait_ge(s_sc, SMS * (c + 1) + 6)
                    wait(act, s_px, NG * (c + 1))
                    nc.scalar.copy(p_hi[:, :, :], sc[:, :, :]).then_inc(s_hi, 1)

            act.wait_ge(s_ln, LN_STEPS + 2)
            act.wait_ge(s_tok, NC)
            over_chunks(nc.scalar, attention)

            act.wait_ge(s_ln, 2 * LN_STEPS + 2)
            nc.scalar.activation(ln_c[:, :], ln_b[:, :], ACT.Sqrt).then_inc(s_lnsq, 1)
            act.wait_ge(s_ln, 2 * LN_STEPS + 4)

            def gate_input(c, par):
                wait(act, s_gT, c - 1)
                normalise(c, par, s_gxn)

            pairs(nc.scalar, gate_input)
            act.wait_ge(s_g, 2)
            nc.scalar.activation(gA[:, :, :], gate[:, :, :], ACT.Exp).then_inc(s_gexp, 1)

            act.wait_ge(s_experts, 64)
            def experts(c):
                for e in range(NE):
                    wait(act, s_y, NE * c + e - 1)
                    for i in range(FC):
                        act.wait_ge(s_h, FC * NE * c + FC * e + i + 1)
                        nc.scalar.activation(hid[e % 2][:, i, :], bank[i][:, 0:CT],
                                             ACT.Gelu_apprx_tanh, bias=b1_sb[:, e, i:i + 1]).then_inc(s_gelu, 1)

            experts(0)
            with nc.scalar.Fori(1, NC) as c:
                experts(c)

        @block.vector
        def _(dve):
            V = nc.vector
            dve.wait_ge(s_bias, 16 * N_BIAS)
            dve.wait_ge(s_par, 16 * N_PAR)
            V.tensor_copy(bias[:, :, :], view(rel_bias, 128, HALF, [1, KS], [0, SUB])).then_inc(s_bn, 1)
            V.tensor_scalar(qb_c, cols[:, 4:5], QSCALE, None, ALU.mult)
            dve.wait_ge(s_bn, 1)
            for n in range(HALF):
                V.tensor_copy(bias[0:32, :, n], rel_bias[0:32, KS - 1 - n:2 * KS - 1 - n])
                V.tensor_copy(bias[32:64, :, SUB - HALF + n], rel_bias[32:64, HALF - 1 - n:HALF - 1 - n + KS])

            def stats(c):
                dve.wait_ge(s_relu, c + 1)
                V.bn_stats(bn_st[:, bass.ds(c, 1), :].rearrange("p a s -> p (a s)"), chan_cols(c)).then_inc(s_bnst, 1)

            stats(0)
            with V.Fori(1, NC - 1) as c:
                stats(c)
            stats(NC - 1)
            dve.wait_ge(s_bnst, NC)
            V.bn_aggr(bn_mv[:, :], bn_st[:, :, :].rearrange("p a s -> p (a s)")).then_inc(s_bnst, 1)
            dve.wait_ge(s_bnst, NC + 1)
            V.tensor_scalar(bn_w[:, 0:1], bn_mv[:, 1:2], EPS, None, ALU.add).then_inc(s_bn, 1)
            dve.wait_ge(s_bnsq, 1)
            V.reciprocal(bn_w[:, 2:3], bn_w[:, 1:2]).then_inc(s_bn, 1)
            dve.wait_ge(s_bn, 3)
            V.tensor_tensor(bn_w[:, 3:4], bn_w[:, 2:3], gamma_c, ALU.mult).then_inc(s_bn, 1)
            dve.wait_ge(s_bn, 4)
            V.tensor_tensor(bn_mv[:, 1:2], bn_mv[:, 0:1], bn_w[:, 3:4], ALU.mult).then_inc(s_bn, 1)
            dve.wait_ge(s_bn, 5)
            V.tensor_tensor(bn_w[:, 0:1], beta_c, bn_mv[:, 1:2], ALU.subtract).then_inc(s_bn, 1)
            dve.wait_ge(s_bn, 6)

            def affine(c, par):
                wait(dve, s_zT, c - 1)
                V.tensor_scalar(zc[par][:, :], chan_cols(c), bn_w[:, 3:4], bn_w[:, 0:1], ALU.mult, ALU.add
                                ).then_inc(s_zc, 1)

            def tile_stats(c):
                for t in range(TPC):
                    i = c * TPC + t
                    ins = V.bn_stats(ln_stats[:, bass.ds(i, 1), :].rearrange("p a s -> p (a s)"),
                                     tokens[:, bass.ds(i, 1), :].rearrange("p a c -> p (a c)"))
                return ins

            def normalise_channels(c, par):
                affine(c, par)
                if not isinstance(c, int) or c > 0:
                    dve.wait_ge(s_tok, c)
                    tile_stats(c - 1).then_inc(s_lnst, 1)

            pairs(V, normalise_channels)
            dve.wait_ge(s_tok, NC)
            tile_stats(NC - 1).then_inc(s_lnst, 1)

            def layer_norm(base, sqrts):
                n = [base]

                def step(ins):
                    n[0] += 1
                    ins.then_inc(s_ln, 1)
                    dve.wait_ge(s_ln, n[0])
                me, ve, mo, vo = (ln_stats[:, :, i] for i in (1, 2, 4, 5))
                step(V.tensor_tensor(ln_a[:, :], me, mo, ALU.subtract))
                step(V.tensor_tensor(ln_b[:, :], ve, vo, ALU.add))
                step(V.tensor_tensor(ln_c[:, :], me, mo, ALU.add))
                step(V.tensor_tensor(ln_a[:, :], ln_a[:, :], ln_a[:, :], ALU.mult))
                step(V.tensor_scalar(ln_b[:, :], ln_b[:, :], 1.0 / C, EPS, ALU.mult, ALU.add))
                step(V.scalar_tensor_tensor(ln_b[:, :], ln_a[:, :], 0.25, ln_b[:, :], ALU.mult, ALU.add))
                step(V.tensor_scalar(ln_a[:, :], ln_c[:, :], -0.5, None, ALU.mult))
                dve.wait_ge(s_lnsq, sqrts)
                step(V.reciprocal(rstd[:, :], ln_c[:, :]))
                step(V.tensor_tensor(nmr[:, :], ln_a[:, :], rstd[:, :], ALU.mult))

            dve.wait_ge(s_lnst, NC)
            layer_norm(0, 1)

            def products(c, par):
                dve.wait_ge(s_qkv, 3 * c + 2)
                wait(dve, s_score, c - 1)
                for b in range(CB):
                    o = L * b
                    V.tensor_tensor(view(qk[par], C, o + HALF, [CT, KS], [1, L - 2 * HALF]),
                                    view(q[par], C, o + HALF, [0, KS], [1, L - 2 * HALF]),
                                    view(k[par], C, o, [1, KS], [1, L - 2 * HALF]), ALU.mult)
                    for t0, k0 in ((o, o), (o + L - HALF, o + L - KS)):
                        ins = V.tensor_tensor(view(qk[par], C, t0, [CT, KS], [1, HALF]),
                                              view(q[par], C, t0, [0, KS], [1, HALF]),
                                              view(k[par], C, k0, [1, KS], [0, HALF]), ALU.mult)
                ins.then_inc(s_qk, 1)

            def softmax(c):
                def step(ins, i):
                    ins.then_inc(s_sc, 1)
                    dve.wait_ge(s_sc, SMS * c + i)
                by_token = [1, SUB], [SUB, KS]
                rows = sc[:, :, :].rearrange("p j n -> p (j n)")
                bias_rows = bias[:, :, :].rearrange("p j n -> p (j n)")
                dve.wait_ge(s_score, c + 1)
                wait(dve, s_hi, c)
                V.tensor_tensor(rows[:, 0:JA * SUB], bank[2][:, 0:JA * SUB], bias_rows[:, 0:JA * SUB], ALU.add)
                step(V.tensor_tensor(rows[:, JA * SUB:], bank[3][:, 0:JB * SUB], bias_rows[:, JA * SUB:], ALU.add), 1)
                step(V.tensor_reduce(mx[:, :], view(sc, 128, 0, *by_token), AX.X, ALU.max), 2)
                step(V.tensor_tensor(sc[:, :, :], sc[:, :, :], view(mx, 128, 0, [0, KS], [1, SUB]), ALU.subtract), 3)
                dve.wait_ge(s_exp, c + 1)
                step(V.tensor_reduce(sm[:, :], view(ex, 128, 0, *by_token), AX.X, ALU.add), 4)
                step(V.reciprocal(rs[:, :], sm[:, :]), 5)
                step(V.scalar_tensor_tensor(sc[:, :, :], ex[:, :, :], PSCALE, view(rs, 128, 0, [0, KS], [1, SUB]),
                                            ALU.mult, ALU.mult), 6)
                dve.wait_ge(s_hi, c + 1)
                V.tensor_tensor(p_lo[:, :, :], sc[:, :, :], p_hi[:, :, :], ALU.subtract).then_inc(s_sc, 1)

            def weigh(c, par):
                wait(dve, s_proj, c)
                for g in range(NG):
                    dve.wait_ge(s_px, NG * c + g + 1)
                    s = g % SPB
                    o = SUB * g
                    lo = HALF if s == 0 else 0
                    hi = SUB - HALF if s == SPB - 1 else SUB
                    start = L * (g // SPB)
                    for j0, nj, b in ((0, JA, 4), (JA, JB, 5)):
                        b += 2 * (g % 2)
                        parts = [(lo, hi - lo, o + lo - HALF, 1)]
                        if s == 0:
                            parts.append((0, HALF, start, 0))
                        if s == SPB - 1:
                            parts.append((hi, HALF, start + L - KS, 0))
                        for n0, nn, v0, step in parts:
                            ins = V.tensor_tensor(view(pv, C, CT * j0 + o + n0, [CT, nj], [1, nn]),
                                                  view(bank[b], C, n0, [SUB, nj], [1, nn]),
                                                  view(v[par], C, v0 + j0, [1, nj], [step, nn]), ALU.mult)
                    ins.then_inc(s_pv, 1)

            def residual(c):
                dve.wait_ge(s_oback, c + 1)
                V.tensor_tensor(tile_rows(tokens, c), bank[0][0:TT, :].rearrange("p (t c) -> p t c", t=TPC),
                                tile_rows(tokens, c), ALU.add).then_inc(s_res, 1)
                dve.wait_ge(s_res, c + 1)
                tile_stats(c).then_inc(s_attn, 1)

            def attention(c, par, inside):
                if inside(0):
                    weigh(c, par)
                if inside(-1):
                    residual(c - 1)
                if inside(2):
                    products(c + 2, par)
                if inside(1):
                    softmax(c + 1)

            over_chunks(V, attention)
            dve.wait_ge(s_attn, NC)
            layer_norm(LN_STEPS + 2, 2)

            def gate_tiles(c, par):
                dve.wait_ge(s_gT, c + 1)
                wait(dve, s_lg, c - 1)
                wait(dve, s_gall, c - 1)
                V.tensor_copy(xnT[par][:, :], bank[par][:, 0:CT]).then_inc(s_gxT, 1)
                dve.wait_ge(s_lg, c + 1)
                V.tensor_tensor(tile_rows(gate, c),
                                bank[2 + par][0:TT, 0:TPC * NE].rearrange("p (t e) -> p t e", t=TPC),
                                view(bg_sb, TT, 0, [0, TPC], [1, NE]), ALU.add).then_inc(s_lgs, 1)

            pairs(V, gate_tiles)

            n = [0]

            def step(ins):
                n[0] += 1
                ins.then_inc(s_g, 1)
                dve.wait_ge(s_g, n[0])

            def per_tile(t):
                return view(t, TT, 0, [1, NT], [0, NE])

            rank = view(expert_rank, TT, 0, [0, NT], [1, NE])
            dve.wait_ge(s_lgs, NC)
            step(V.tensor_reduce(ln_a[:, :], gate[:, :, :], AX.X, ALU.max))
            step(V.tensor_tensor(gate[:, :, :], gate[:, :, :], per_tile(ln_a), ALU.subtract))
            dve.wait_ge(s_gexp, 1)
            step(V.tensor_reduce(ln_b[:, :], gA[:, :, :], AX.X, ALU.add))
            step(V.reciprocal(ln_c[:, :], ln_b[:, :]))
            step(V.tensor_tensor(gA[:, :, :], gA[:, :, :], per_tile(ln_c), ALU.mult))

            def largest(values, hot):
                step(V.tensor_reduce(ln_a[:, :], values[:, :, :], AX.X, ALU.max))
                step(V.tensor_tensor(hot[:, :, :], values[:, :, :], per_tile(ln_a), ALU.is_equal))
                step(V.tensor_tensor(hot[:, :, :], hot[:, :, :], rank, ALU.mult))
                step(V.tensor_reduce(ln_a[:, :], hot[:, :, :], AX.X, ALU.max))
                step(V.tensor_tensor(hot[:, :, :], rank, per_tile(ln_a), ALU.is_equal))

            largest(gA, gate)
            step(V.scalar_tensor_tensor(gB[:, :, :], gate[:, :, :], -2.0, gA[:, :, :], ALU.mult, ALU.add))
            largest(gB, gC)
            step(V.tensor_tensor(gate[:, :, :], gate[:, :, :], gC[:, :, :], ALU.add))
            step(V.tensor_tensor(gate[:, :, :], gate[:, :, :], gA[:, :, :], ALU.mult))

            def experts(c):
                for e in range(NE):
                    y = view(ysum, TT, (e % 2) * FF, [C, TPC], [1, C])
                    dve.wait_ge(s_y, NE * c + e + 1)
                    V.tensor_tensor(y, bank[4 + e % 2][0:TT, :].rearrange("p (t c) -> p t c", t=TPC),
                                    view(b2_sb, TT, C * e, [0, TPC], [1, C]), ALU.add).then_inc(s_yb, 1)
                    dve.wait_ge(s_yb, NE * c + e + 1)
                    wait(dve, s_acc, NE * c + e)
                    for t in range(TPC):
                        i = c * TPC + t
                        row = tokens[:, bass.ds(i, 1), :].rearrange("p a c -> p (a c)")
                        ins = V.scalar_tensor_tensor(row, view(ysum, TT, (e % 2) * FF + C * t, [1, C]),
                                                     gate[:, bass.ds(i, 1), e], row, ALU.mult, ALU.add)
                    ins.then_inc(s_acc, 1)

            experts(0)
            with V.Fori(1, NC) as c:
                experts(c)


_INS = ["x", "L0_tok_W", "L0_tok_b", "L0_tok_gamma", "L0_tok_beta", "L0_attn_qkv_w", "L0_attn_qkv_b",
        "L0_attn_rpb", "L0_attn_proj_w", "L0_attn_proj_b", "L0_ffn_Wg", "L0_ffn_bg", "L0_ffn_W1", "L0_ffn_b1",
        "L0_ffn_W2", "L0_ffn_b2"]


def kernel(**inputs):
    import numpy as _np
    import concourse.bacc as _bacc
    from concourse import mybir as _mybir
    from concourse.bass_utils import run_bass_kernel_spmd as _run

    nc = _bacc.Bacc("TRN2", target_bir_lowering=False, num_devices=1)
    arrays, args = {}, []
    for name in _INS:
        a = _np.ascontiguousarray(inputs[name])
        arrays[f"in_{name}_dram"] = a
        args.append(nc.dram_tensor(f"in_{name}_dram", a.shape, _mybir.dt.from_np(a.dtype), kind="ExternalInput").ap())
    out = nc.dram_tensor("out_dram", (B, L, C), F32, kind="ExternalOutput").ap()
    tower(nc, *args, out)
    r = _run(nc, [arrays], core_ids=[0])
    return r.results[0]["out_dram"]
```

```python
import concourse.bass as bass
from concourse import mybir
from concourse.alu_op_type import AluOpType as ALU
from contextlib import ExitStack

F32 = mybir.dt.float32
F16 = mybir.dt.float16
I32 = mybir.dt.int32
ACT = mybir.ActivationFunctionType
AX = mybir.AxisListType

B, S, D = 32, 256, 64
TAPS = 5
L = S - TAPS + 1
C = 128
NTOK = B * L
HEADS, HD = 16, 8
KS = 13
HALF = KS // 2
NE, FF = 8, 512
FC = FF // C
EPS = 1e-5
QSCALE = float(HD) ** -0.5

CB = 2
CT = CB * L
NC = B // CB
TT = 126
TPC = CT // TT
NT = NC * TPC
SUB = 63
NG = CT // SUB
JA = 8
JB = KS - JA
SPB = L // SUB
TOP = 2
BLK = 384
SPT = BLK // 128
NB = (TOP * NTOK + NE * (BLK - 1)) // BLK
REGION = NTOK + BLK
META = 4
ROW = C + META
MAXB = -(-NTOK // BLK)
XSCALE = 64.0
WSCALE = 64.0
HSCALE = 16.0
PSCALE = 16384.0

ROWS = {0: 0, SPB: 1, SPB - 1: 2, 2 * SPB - 1: 3}
for _g in range(NG):
    if _g not in ROWS:
        ROWS[_g] = len(ROWS)


def view(t, parts, offset, *dims, part0=0):
    row = 1
    for n in t.shape[1:]:
        row *= n
    return bass.AP(tensor=t[:].tensor, offset=offset + part0 * row, ap=[[row, parts], *[list(d) for d in dims]])


def tower(nc, x, tok_W, tok_b, tok_gamma, tok_beta, qkv_w, qkv_b, rpb, proj_w, proj_b,
          Wg, bg, W1, b1, W2, b2, out):
    ctx = ExitStack()
    with ctx:
        def sb(name, shape, dt=F32):
            return ctx.enter_context(nc.sbuf_tensor(name, shape, dt))

        def sem(name):
            return ctx.enter_context(nc.semaphore(name))

        ident = sb("ident", [128, 128])
        head_window = sb("head_window", [128, 240])
        head_expand = sb("head_expand", [128, NG, 128], F16)
        rel_bias = sb("rel_bias", [128, 2 * KS - 1])
        bias = sb("bias", [128, KS, SUB])
        w_nat = sb("w_nat", [C, TAPS * D])
        w_tap = sb("w_tap", [128, 3, C])
        qkv_sb = sb("qkv_sb", [C, 3 * C])
        proj_sb = sb("proj_sb", [C, C])
        wg_sb = sb("wg_sb", [C, NE])
        bg_sb = sb("bg_sb", [TT, NE])
        b2_sb = sb("b2_sb", [128, NE, C])
        vec_nat = sb("vec_nat", [7 + NE * FC, C])
        cols = sb("cols", [C, 8 + NE * FC])
        tok_b_c, gamma_c, beta_c, proj_b_c = (cols[:, i:i + 1] for i in range(4))
        qkv_b_c = cols[:, 4:7]
        b1_c = cols[:, 7:7 + NE * FC]
        qb_c = cols[:, 7 + NE * FC:8 + NE * FC]
        before = sb("before", [TT, TT], F16)
        ones16 = sb("ones16", [TT, TT], F16)
        expert_rank = sb("expert_rank", [TT, NE])
        region = sb("region", [TT, NE])
        minus_half = sb("minus_half", [TT, TPC])
        result_row = sb("result_row", [TT, TOP, NT], I32)
        pad = sb("pad", [128, SPT, ROW])

        chan = sb("chan", [C, NTOK])
        tokens = sb("tokens", [TT, NT, C])
        ids = [sb(f"ids{i}", [128, SPT], I32) for i in range(4)]
        ln_stats = sb("ln_stats", [TT, NT, 6])
        ln_a = sb("ln_a", [TT, NT])
        ln_b = sb("ln_b", [TT, NT])
        ln_c = sb("ln_c", [TT, NT])
        rstd = sb("rstd", [TT, NT])
        nmr = sb("nmr", [TT, NT])
        bn_st = sb("bn_st", [C, NC, 6])
        bn_mv = sb("bn_mv", [C, 2])
        bn_w = sb("bn_w", [C, 4])

        xn = [sb(f"xn{i}", [TT, TPC, C]) for i in range(2)]
        xnT = [sb(f"xnT{i}", [C, CT]) for i in range(2)]
        zc = xnT
        q = [sb(f"q{i}", [C, CT]) for i in range(2)]
        k = [sb(f"k{i}", [C, CT]) for i in range(2)]
        v = [sb(f"v{i}", [C, CT]) for i in range(2)]
        qk = [sb(f"qk{i}", [C, KS, CT]) for i in range(2)]
        xin = [view(qk[1], 128, i * 8 * D, [2 * D, 4], [1, 2 * D]) for i in range(4)]
        xT = [view(qk[1], 128, 32 * D + i * CB * S, [1, CB * S]) for i in range(2)]
        pv = chan
        ysum = sb("ysum", [TT, 2, FF])
        w1_sb = view(qk[0], C, FC * CT, [FF, NE], [1, FF])
        w2_sb = view(qk[1], C, FC * CT, [FF, NE], [C, FC], [1, C])
        sc = sb("sc", [128, KS, SUB])
        ex = sb("ex", [128, KS, SUB])
        mx = sb("mx", [128, SUB])
        sm = sb("sm", [128, SUB])
        rs = sb("rs", [128, SUB])
        p_hi = sb("p_hi", [128, KS, SUB], F16)
        p_lo = sb("p_lo", [128, KS, SUB], F16)
        oT = sb("oT", [C, CT])

        gst = [sb(f"gst{i}", [TT, TPC, 6]) for i in range(2)]
        gln = sb("gln", [TT, 8, TPC])
        grstd = [sb(f"grstd{i}", [TT, TPC]) for i in range(2)]
        gnmr = [sb(f"gnmr{i}", [TT, TPC]) for i in range(2)]
        xrow = [sb(f"xrow{i}", [TT, TPC, ROW]) for i in range(2)]
        gxT = sb("gxT", [C, CT])
        lg = sb("lg", [TT, TPC, NE])
        pr = sb("pr", [TT, TPC, NE])
        hot = sb("hot", [TT, TOP, TPC, NE])
        hit = sb("hit", [TT, TOP, TPC, NE])
        slot = sb("slot", [TT, TPC, NE])
        pos = sb("pos", [TT, TOP, TPC])
        idx = [sb(f"idx{i}", [TT, TOP, TPC], I32) for i in range(2)]
        gm = sb("gm", [TT, TPC])
        gs = sb("gs", [TT, TPC])
        chosen = sb("chosen", [TT, TPC, NE], F16)
        counted = sb("counted", [TT, NE], F16)
        fresh = sb("fresh", [TT, NE], F16)
        top = sb("top", [TT, TOP, TPC])
        weight = sb("weight", [TT, TOP, NT])

        tb_n = sb("tb_n", [TT, NE])
        tb_k = sb("tb_k", [1, NE, MAXB])
        tb_thr = sb("tb_thr", [1, NE, MAXB])
        tb_tri = sb("tb_tri", [1, NE, NE])
        tb_tmp = sb("tb_tmp", [1, NE, NE])
        tb_blocks = sb("tb_blocks", [1, NE])
        tb_ends = sb("tb_ends", [1, NE])
        tb_id = sb("tb_id", [1, NB])
        tb_past = sb("tb_past", [1, NB, NE])
        tb_e = sb("tb_e", [1, NB])
        tb_s = sb("tb_s", [1, NB])
        tb_u = sb("tb_u", [1, NB])
        tab_e = sb("tab_e", [1, NB], I32)
        tab_row = sb("tab_row", [1, NB], I32)
        tab_pad = sb("tab_pad", [1, NE], I32)

        wst = sb("wst", [C, FF])
        wst_hi = sb("wst_hi", [C, FF], F16)
        wst_lo = sb("wst_lo", [C, FF], F16)
        NW = NE * FF
        halves0 = view(qk[0], C, 0, [1, 3 * NW // 2]).bitcast(F16)
        halves1 = view(qk[1], C, 0, [1, NW // 2]).bitcast(F16)
        w1_hi, w1_lo, w2_hi, w2_lo = halves0[:, 0:NW], halves0[:, NW:2 * NW], halves0[:, 2 * NW:3 * NW], halves1
        xb = [sb(f"xb{i}", [128, SPT, ROW]) for i in range(4)]
        xh = [sb(f"xh{i}", [C, BLK], F16) for i in range(2)]
        xl = [sb(f"xl{i}", [C, BLK], F16) for i in range(2)]
        FB = FC * BLK
        act32 = [view(chan, C, i * FB, [1, FB]) for i in range(2)]
        act_hi = [view(chan, C, 2 * FB + i * FB, [1, FB // 2]).bitcast(F16) for i in range(2)]
        act_lo = [view(chan, C, 2 * FB + i * FB + FB // 2, [1, FB // 2]).bitcast(F16) for i in range(2)]
        ys = [sb(f"ys{i}", [128, SPT, C]) for i in range(2)]
        comb = [view(qk[1], TT, NW // 2 + i * TOP * TPC * C, [TPC * C, TOP], [1, TPC * C]) for i in range(4)]

        slots = nc.dram_tensor("slots", (NE * REGION + BLK, ROW), F32, kind="Internal").ap()
        results = nc.dram_tensor("results", (TOP * NTOK, C), F32, kind="Internal").ap()
        w_halves = nc.dram_tensor("w_halves", (4, C, NE, FF), F16, kind="Internal").ap()

        bank = [ctx.enter_context(nc.psum_tensor(f"bank{i}", [128, 512], F32)) for i in range(8)]

        s_par = sem("s_par")
        s_w = sem("s_w")
        s_const = sem("s_const")
        s_wT = sem("s_wT")
        s_wtap = sem("s_wtap")
        s_bias = sem("s_bias")
        s_xin = [sem(f"s_xin{i}") for i in range(4)]
        s_xtail = sem("s_xtail")
        s_xTp = sem("s_xTp")
        s_xT = sem("s_xT")
        s_conv = sem("s_conv")
        s_relu = sem("s_relu")
        s_bnst = sem("s_bnst")
        s_bn = sem("s_bn")
        s_bnsq = sem("s_bnsq")
        s_zc = sem("s_zc")
        s_zT = sem("s_zT")
        s_tok = sem("s_tok")
        s_lnst = sem("s_lnst")
        s_ln = sem("s_ln")
        s_lnsq = sem("s_lnsq")
        s_xn = sem("s_xn")
        s_xnTp = sem("s_xnTp")
        s_xnT = sem("s_xnT")
        s_qkvp = sem("s_qkvp")
        s_qkv = sem("s_qkv")
        s_qk = sem("s_qk")
        s_score = sem("s_score")
        s_sc = sem("s_sc")
        s_exp = sem("s_exp")
        s_hi = sem("s_hi")
        s_px = sem("s_px")
        s_pv = sem("s_pv")
        s_proj = sem("s_proj")
        s_oT = sem("s_oT")
        s_oback = sem("s_oback")
        s_res = sem("s_res")
        s_g = sem("s_g")
        s_gexp = sem("s_gexp")
        s_gconst = sem("s_gconst")
        s_vecs = sem("s_vecs")
        s_cols = sem("s_cols")
        s_gstat = sem("s_gstat")
        s_gln = sem("s_gln")
        s_xrow = sem("s_xrow")
        s_gT = sem("s_gT")
        s_gxT = sem("s_gxT")
        s_lg = sem("s_lg")
        s_rank = sem("s_rank")
        s_pr = sem("s_pr")
        s_hot = sem("s_hot")
        s_slot = sem("s_slot")
        s_meta = sem("s_meta")
        s_scat = sem("s_scat")
        s_weight = sem("s_weight")
        s_total = sem("s_total")
        s_table = sem("s_table")
        s_pads = sem("s_pads")
        s_wld = sem("s_wld")
        s_wsplit = sem("s_wsplit")
        s_wst = sem("s_wst")
        s_whalves = sem("s_whalves")
        s_xb = [sem(f"s_xb{i}") for i in range(4)]
        s_xbT = sem("s_xbT")
        s_xh = sem("s_xh")
        s_xl = sem("s_xl")
        s_ids = sem("s_ids")
        s_h = sem("s_h")
        s_gelu = sem("s_gelu")
        s_hi32 = sem("s_hi32")
        s_split = sem("s_split")
        s_y = sem("s_y")
        s_ev = sem("s_ev")
        s_ysc = [sem(f"s_ysc{i}") for i in range(2)]
        s_comb = [sem(f"s_comb{i}") for i in range(4)]
        s_first = sem("s_first")
        s_acc = sem("s_acc")
        s_passed = sem("s_passed")
        s_out = sem("s_out")

        block = ctx.enter_context(nc.Block())

        def wait(eng, semaphore, value):
            if isinstance(value, int) and value <= 0:
                return
            eng.wait_ge(semaphore, value)

        def valid(c):
            return not isinstance(c, int) or 0 <= c < NC

        def pairs(engine, body):
            body(0, 0)
            body(1, 1)
            with engine.Fori(1, NC // 2) as p:
                for par in range(2):
                    body(2 * p + par, par)

        def over_chunks(engine, body):
            def fixed(c):
                body(c, c % 2, lambda d: 0 <= c + d < NC)
            for c in range(-3, 4):
                fixed(c)
            with engine.Fori(2, (NC - 4) // 2) as p:
                for par in range(2):
                    body(2 * p + par, par, lambda d: True)
            for c in range(NC - 4, NC + 3):
                fixed(c)

        def over_blocks(engine, body):
            def fixed(b):
                body(b, b % 4, lambda d: 0 <= b + d < NB)
            last = (NB - 3) // 4 * 4
            for b in range(-3, 4):
                fixed(b)
            with engine.Fori(1, last // 4) as p:
                for u in range(4):
                    body(4 * p + u, u, lambda d: True)
            for b in range(last, NB + 2):
                fixed(b)

        def sent(b, par):
            return 8 * SPT * (b - par) + 16 * SPT

        def wait_alone(eng, semaphore, value):
            wait(eng, semaphore, value)
            if not isinstance(value, int):
                eng.sem_inc(s_passed, 1)

        def tile_rows(t, c):
            return t[:, bass.ds(c * TPC, TPC), :]

        def chan_cols(c):
            return chan[:, bass.ds(c * CT, CT)]

        x_flat = x.rearrange("b s d -> (b s) d")
        out_flat = out.rearrange("b t c -> (b t) c")

        N_PAR = 5
        N_GCONST = 16
        TABLE = 15
        RANKS = 320
        GLN = 10
        GS = 16
        SLS = 6
        ROUTES = 16 * TOP * TPC
        SMS = 7
        LN_STEPS = 7
        N_BIAS = NG

        @block.sync
        def _(sp):
            def load_x(c, buf, tiles=4):
                sp.dma_start(xin[buf][:, 0:tiles, :],
                             bass.AP(tensor=x.tensor, offset=c * CB * S * D, ap=[[D, 128], [128 * D, tiles], [1, 2 * D]])
                             ).then_inc(s_xin[buf], 16)

            sp.dma_start(w_nat[:, :], tok_W).then_inc(s_w, 16)
            for c in range(4):
                load_x(c, c)
            for i, vec in enumerate((tok_b, tok_gamma, tok_beta, proj_b)):
                sp.dma_start(vec_nat[i:i + 1, :], vec.rearrange("(a p) -> a p", a=1)).then_inc(s_vecs, 16)
            sp.dma_start(vec_nat[4:7, :], qkv_b.rearrange("(a p) -> a p", p=C)).then_inc(s_vecs, 16)
            sp.dma_start(vec_nat[7:7 + NE * FC, :], b1.rearrange("e (i f) -> (e i) f", f=C)).then_inc(s_vecs, 16)
            sp.dma_start(b2_sb[:, :, :], b2.partition_broadcast(128)).then_inc(s_par, 16)
            sp.dma_start(qkv_sb[:, :], qkv_w).then_inc(s_par, 16)
            sp.dma_start(proj_sb[:, :], proj_w).then_inc(s_par, 16)
            sp.dma_start(wg_sb[:, :], Wg).then_inc(s_par, 16)
            sp.dma_start(bg_sb[:, :], bg.partition_broadcast(TT)).then_inc(s_par, 16)
            for r in range(NG):
                sp.dma_start(rel_bias[16 * r:16 * r + 16, :], rpb).then_inc(s_bias, 16)
            with nc.sync.Fori(1, NC // 4 - 1) as p:
                for u in range(4):
                    c = 4 * p + u
                    sp.wait_ge(s_xTp, c - 3)
                    load_x(c, u)
            for u in range(4):
                c = NC - 4 + u
                sp.wait_ge(s_xTp, c - 3)
                if c == NC - 1:
                    row = B * S - 128
                    sp.dma_start(xin[u][0:127, 3, :], bass.AP(tensor=x.tensor, offset=row * D, ap=[[D, 127], [1, 2 * D]])
                                 ).then_inc(s_xtail, 16)
                    sp.dma_start(xin[u][127:128, 3, 0:D], x_flat[B * S - 1:B * S, :]).then_inc(s_xtail, 16)
                    sp.wait_ge(s_xtail, 32)
                load_x(c, u, 3 if c == NC - 1 else 4)
            sp.wait_ge(s_score, NC)
            sp.wait_ge(s_wst, 64 * NE)
            sp.dma_start(halves0[:, :].rearrange("c (h n) -> c h n", h=3),
                         w_halves[0:3].rearrange("h c e f -> c h (e f)")).then_inc(s_whalves, 16)
            sp.dma_start(halves1[:, :], w_halves[3].rearrange("c e f -> c (e f)")).then_inc(s_whalves, 16)
            sp.wait_ge(s_gconst, N_GCONST)
            sp.dma_start(slots[NE * REGION:NE * REGION + BLK, :].rearrange("(k p) c -> p k c", p=128), pad[:, :, :]
                         ).then_inc(s_pads, 16)
            sp.wait_ge(s_table, TABLE)
            for e in range(NE):
                row = nc.sync.value_load(tab_pad[0:1, e:e + 1], min_val=0, max_val=NE * REGION - BLK)
                sp.dma_start(slots[bass.ds(row, BLK), :].rearrange("(k p) c -> p k c", p=128), pad[:, :, :]
                             ).then_inc(s_pads, 16)

            def fetch(c, u):
                for j in range(TOP):
                    sp.dma_start(comb[u][:, j, :].rearrange("p (t c) -> p t c", t=TPC),
                                 results[bass.ds(c * CT + j * NTOK, CT), :].rearrange("(t p) c -> p t c", p=TT)
                                 ).then_inc(s_comb[u], 16)

            def store(c):
                sp.wait_ge(s_acc, c + 1)
                sp.dma_start(out_flat[bass.ds(c * CT, CT), :].rearrange("(k p) c -> p k c", p=TT),
                             tile_rows(tokens, c)).then_inc(s_out, 16)

            for par in range(2):
                sp.wait_ge(s_ysc[par], sent((NB - 1 - par) // 2 * 2 + par, par))
            for c in range(4):
                fetch(c, c)
            with nc.sync.Fori(0, NC // 4 - 1) as p:
                for u in range(4):
                    store(4 * p + u)
                    fetch(4 * p + u + 4, u)
            for c in range(NC - 4, NC):
                store(c)
            sp.wait_ge(s_out, 16 * NC)

        @block.gpsimd
        def _(pool):
            pool.memset(ident[:, :], 0.0).then_inc(s_const, 1)
            pool.memset(head_window[:, :], 0.0).then_inc(s_const, 1)
            pool.memset(head_expand[:, :, :], 0.0).then_inc(s_const, 1)
            wait_alone(pool, s_const, 3)
            pool.affine_select(out=ident[:, :], in_=ident[:, :], compare_op=ALU.not_equal, fill=1.0,
                               base=0, pattern=[[-1, 128]], channel_multiplier=1).then_inc(s_const, 1)
            pool.memset(head_window[:, 112:128], 1.0).then_inc(s_const, 1)
            pool.affine_select(out=head_expand[:, :, :], in_=head_expand[:, :, :], compare_op=ALU.not_equal,
                               fill=1.0, base=0, pattern=[[-16, NG], [-1, HEADS], [0, HD]],
                               channel_multiplier=1).then_inc(s_const, 1)
            wait_alone(pool, s_const, 6)
            pool.affine_select(out=head_window[:, 112:128], in_=head_window[:, 112:128], compare_op=ALU.is_ge,
                               fill=0.0, base=0, pattern=[[-HD, HEADS]], channel_multiplier=1).then_inc(s_const, 1)
            wait_alone(pool, s_const, 7)
            pool.affine_select(out=head_window[:, 112:128], in_=head_window[:, 112:128], compare_op=ALU.is_ge,
                               fill=0.0, base=HD - 1, pattern=[[HD, HEADS]], channel_multiplier=-1).then_inc(s_const, 1)
            G = nc.gpsimd
            G.iota(expert_rank[:, :], pattern=[[-1, NE]], base=NE, channel_multiplier=0,
                   allow_small_or_imprecise_dtypes=True).then_inc(s_gconst, 1)
            G.iota(region[:, :], pattern=[[REGION, NE]], base=0, channel_multiplier=0,
                   allow_small_or_imprecise_dtypes=True).then_inc(s_gconst, 1)
            G.iota(tb_thr[:, :, :], pattern=[[0, NE], [BLK, MAXB]], base=0, channel_multiplier=0,
                   allow_small_or_imprecise_dtypes=True).then_inc(s_gconst, 1)
            G.iota(tb_id[:, :], pattern=[[1, NB]], base=0, channel_multiplier=0,
                   allow_small_or_imprecise_dtypes=True).then_inc(s_gconst, 1)
            G.iota(result_row[:, :, :], pattern=[[NTOK, TOP], [TT, NT]], base=0, channel_multiplier=1
                   ).then_inc(s_gconst, 1)
            G.memset(minus_half[:, :], -0.5).then_inc(s_gconst, 1)
            G.memset(ones16[:, :], 1.0).then_inc(s_gconst, 1)
            G.memset(before[:, :], 1.0).then_inc(s_gconst, 1)
            G.memset(counted[:, :], 0.0).then_inc(s_gconst, 1)
            G.memset(tb_tri[:, :, :], 1.0).then_inc(s_gconst, 1)
            G.memset(pad[:, :, :], 0.0).then_inc(s_gconst, 1)
            for i in range(2):
                G.memset(xrow[i][:, :, C:ROW], 0.0).then_inc(s_gconst, 1)
            wait_alone(pool, s_gconst, 13)
            G.iota(pad[:, :, C:C + 1].bitcast(I32), pattern=[[0, SPT], [0, 1]], base=TOP * NTOK, channel_multiplier=0
                   ).then_inc(s_gconst, 1)
            pool.affine_select(out=before[:, :], in_=before[:, :], compare_op=ALU.is_ge, fill=0.0, base=-1,
                               pattern=[[1, TT]], channel_multiplier=-1).then_inc(s_gconst, 1)
            pool.affine_select(out=tb_tri[:, :, :], in_=tb_tri[:, :, :], compare_op=ALU.is_ge, fill=0.0, base=0,
                               pattern=[[1, NE], [-1, NE]], channel_multiplier=0).then_inc(s_gconst, 1)
            wait_alone(pool, s_gconst, N_GCONST)

            with nc.gpsimd.Fori(0, NE) as e:
                for m, (w, hi) in enumerate(((W1, 0), (W2, 2))):
                    n = 2 * e + m
                    if m:
                        src = w[bass.ds(e, 1)].rearrange("a (i p) c -> p (a i) c", p=C)
                    else:
                        src = w[bass.ds(e, 1)].rearrange("a c f -> c (a f)").rearrange("c (i f) -> c i f", i=FC)
                    pool.dma_start(wst[:, :].rearrange("p (i c) -> p i c", i=FC), src).then_inc(s_wld, 16)
                    wait_alone(pool, s_wld, 16 * n + 16)
                    nc.gpsimd.tensor_scalar(wst[:, :], wst[:, :], WSCALE, None, ALU.mult).then_inc(s_wsplit, 1)
                    wait_alone(pool, s_wsplit, 3 * n + 1)
                    nc.gpsimd.tensor_copy(wst_hi[:, :], wst[:, :]).then_inc(s_wsplit, 1)
                    wait_alone(pool, s_wsplit, 3 * n + 2)
                    nc.gpsimd.tensor_tensor(wst_lo[:, :], wst[:, :], wst_hi[:, :], ALU.subtract).then_inc(s_wsplit, 1)
                    wait_alone(pool, s_wsplit, 3 * n + 3)
                    for j, half in enumerate((wst_hi, wst_lo)):
                        pool.dma_start(w_halves[hi + j, :, bass.ds(e, 1), :].rearrange("c a f -> c (a f)"), half[:, :]
                                       ).then_inc(s_wst, 16)
                    wait_alone(pool, s_wst, 32 * n + 32)

            def second_norm(g, par):
                def step(ins, i):
                    ins.then_inc(s_gln, 1)
                    wait_alone(pool, s_gln, GLN * g + i)
                me, ve, mo, vo = (gst[par][:, :, i] for i in (1, 2, 4, 5))
                wait_alone(pool, s_gstat, g + 1)
                wait_alone(pool, s_xrow, g - 1)
                step(G.tensor_tensor(gln[:, 0, :], me, mo, ALU.subtract), 1)
                step(G.tensor_tensor(gln[:, 1, :], ve, vo, ALU.add), 2)
                step(G.tensor_tensor(gln[:, 2, :], me, mo, ALU.add), 3)
                step(G.tensor_tensor(gln[:, 3, :], gln[:, 0, :], gln[:, 0, :], ALU.mult), 4)
                step(G.tensor_scalar(gln[:, 4, :], gln[:, 1, :], 1.0 / C, EPS, ALU.mult, ALU.add), 5)
                step(G.tensor_scalar(gln[:, 5, :], gln[:, 3, :], 0.25, None, ALU.mult), 6)
                step(G.tensor_tensor(gln[:, 6, :], gln[:, 4, :], gln[:, 5, :], ALU.add), 7)
                step(G.tensor_tensor(grstd[par][:, :], gln[:, 6, :], minus_half[:, :], ALU.pow), 8)
                step(G.tensor_scalar(gln[:, 7, :], gln[:, 2, :], -0.5, None, ALU.mult), 9)
                step(G.tensor_tensor(gnmr[par][:, :], gln[:, 7, :], grstd[par][:, :], ALU.mult), 10)

            def send(g, par):
                wait_alone(pool, s_g, GS * g + GS)
                G.tensor_copy(weight[:, :, bass.ds(g * TPC, TPC)], top[:, :, :]).then_inc(s_weight, 1)
                wait_alone(pool, s_slot, SLS * g + 4)
                for j in range(TOP):
                    wait_alone(pool, s_scat, ROUTES * g + j * (ROUTES // 2))
                    G.tensor_copy(xrow[par][:, :, C:C + 1].bitcast(I32).rearrange("p t a -> p (t a)"),
                                  result_row[:, j, bass.ds(g * TPC, TPC)]).then_inc(s_meta, 1)
                    wait_alone(pool, s_meta, TOP * g + j + 1)
                    for t in range(TPC):
                        pool.indirect_dma_start(
                            out=slots, out_offset=bass.IndirectOffsetOnAxis(ap=idx[par][:, j, t:t + 1], axis=0),
                            in_=xrow[par][:, t, :], in_offset=None).then_inc(s_scat, 16)

            def attention(c, par, inside):
                if inside(-3):
                    send(c - 3, 1 - par)
                if inside(-1):
                    second_norm(c - 1, 1 - par)

            over_chunks(nc.gpsimd, attention)

            def experts(b, u, inside):
                if inside(-1):
                    wait_alone(pool, s_ev, b)
                    for k in range(SPT):
                        pool.indirect_dma_start(
                            out=results, out_offset=bass.IndirectOffsetOnAxis(ap=ids[(u - 1) % 4][:, k:k + 1], axis=0),
                            in_=ys[(u - 1) % 2][:, k, :], in_offset=None,
                            bounds_check=TOP * NTOK - 1, oob_is_err=False).then_inc(s_ysc[(u - 1) % 2], 16)

            over_blocks(nc.gpsimd, experts)

        @block.tensor
        def _(pe):
            pe.wait_ge(s_w, 16)
            pe.wait_ge(s_const, 4)
            nc.tensor.transpose(bank[7][:, 0:128], w_nat[:, 0:128], ident[:, :])
            nc.tensor.transpose(bank[7][:, 128:256], w_nat[:, 128:256], ident[:, :])
            nc.tensor.transpose(bank[7][0:64, 256:384], w_nat[:, 256:320], ident[:, :]).then_inc(s_wT, 1)
            pe.wait_ge(s_vecs, 96)
            nc.tensor.transpose(bank[6][:, 0:7 + NE * FC], vec_nat[:, :], ident[0:7 + NE * FC, 0:7 + NE * FC]
                                ).then_inc(s_cols, 1)
            pe.wait_ge(s_wtap, 1)

            def frames(c, buf, par):
                wait(pe, s_xT, c - 1)
                for t in range(4):
                    ins = nc.tensor.transpose(bank[par][:, 128 * t:128 * t + 128], xin[buf][:, t, :], ident[:, :])
                ins.then_inc(s_xTp, 1)

            def conv(c, par):
                pe.wait_ge(s_xT, c + 1)
                wait(pe, s_relu, c - 1)
                acc = bank[2 + par][:, 0:CT].rearrange("o (b t) -> o b t", b=CB)
                xv = xT[par][:, :].rearrange("p (b s) -> p b s", b=CB)
                nc.tensor.matmul(acc, w_tap[:, 0, :], xv[:, :, 0:L], start=True, stop=False)
                nc.tensor.matmul(acc, w_tap[:, 1, :], xv[:, :, 2:2 + L], start=False, stop=False)
                nc.tensor.matmul(acc, w_tap[0:64, 2, :], xv[0:64, :, 4:4 + L], start=False, stop=True
                                 ).then_inc(s_conv, 1)

            pe.wait_ge(s_xin[0], 16)
            frames(0, 0, 0)
            for c in range(1, 4):
                pe.wait_ge(s_xin[c], 16)
                frames(c, c, c % 2)
                conv(c - 1, (c - 1) % 2)
            with nc.tensor.Fori(1, NC // 4) as p:
                for u in range(4):
                    c = 4 * p + u
                    pe.wait_ge(s_xin[u], 16 * p + 16)
                    frames(c, u, u % 2)
                    conv(c - 1, (u - 1) % 2)
            conv(NC - 1, (NC - 1) % 2)

            def tiles(c, par):
                pe.wait_ge(s_zc, c + 1)
                wait(pe, s_tok, c - 1)
                for t in range(TPC):
                    ins = nc.tensor.transpose(bank[par][0:TT, C * t:C * t + C],
                                              zc[par][:, TT * t:TT * t + TT], ident[:, :])
                ins.then_inc(s_zT, 1)

            pairs(nc.tensor, tiles)

            def transposes(c, par):
                pe.wait_ge(s_xn, c + 1)
                wait(pe, s_res, c - 3)
                wait(pe, s_g, GS * (c - 5) + 1)
                for t in range(TPC):
                    ins = nc.tensor.transpose(bank[0][:, TT * t:TT * t + TT], xn[par][:, t, :], ident[0:TT, 0:TT])
                ins.then_inc(s_xnTp, 1)

            def qkv(c, par):
                pe.wait_ge(s_xnT, c + 1)
                wait(pe, s_oT, c - 2)
                for i, b in enumerate((1, 0, 1)):
                    if i == 2:
                        pe.wait_ge(s_qkv, 3 * c + 1)
                    nc.tensor.matmul(bank[b][:, 0:CT], qkv_sb[:, C * i:C * i + C], xnT[par][:, :],
                                     start=True, stop=True).then_inc(s_qkvp, 1)

            def scores(c, par):
                pe.wait_ge(s_qk, c + 1)
                wait(pe, s_sc, SMS * (c - 1) + 1)
                add_heads(0, JA, 2, par)

            def scores_rest(c, par):
                wait(pe, s_slot, SLS * (c - 4) + 1)
                add_heads(JA, JB, 3, par).then_inc(s_score, 1)

            def add_heads(j0, nj, b, par):
                for g in range(NG):
                    col = 112 - 16 * ROWS[g]
                    ins = nc.tensor.matmul(bank[b][:, 0:nj * SUB].rearrange("p (j n) -> p j n", j=nj),
                                           head_window[:, col:col + 128],
                                           qk[par][:, j0:j0 + nj, SUB * g:SUB * g + SUB],
                                           start=(g == 0), stop=(g == NG - 1))
                return ins

            def spread(c):
                pe.wait_ge(s_hi, c + 1)
                pe.wait_ge(s_sc, SMS * c + SMS)
                for g in range(NG):
                    wait(pe, s_pv, NG * c + g - 1)
                    for j0, nj, b in ((0, JA, 4), (JA, JB, 5)):
                        dst = bank[b + 2 * (g % 2)][:, 0:nj * SUB]
                        lhsT = head_expand[:, ROWS[g], :]
                        nc.tensor.matmul(dst, lhsT, p_hi[:, j0:j0 + nj, :].rearrange("p j n -> p (j n)"),
                                         start=True, stop=False)
                        ins = nc.tensor.matmul(dst, lhsT, p_lo[:, j0:j0 + nj, :].rearrange("p j n -> p (j n)"),
                                               start=False, stop=True)
                    ins.then_inc(s_px, 1)

            def project(c):
                pe.wait_ge(s_pv, NG * c + NG)
                if valid(c + 2):
                    pe.wait_ge(s_qkv, 3 * (c + 2) + 3)
                wait(pe, s_oT, c)
                for j in range(KS):
                    ins = nc.tensor.matmul(bank[1][:, 0:CT], proj_sb[:, :], pv[:, CT * j:CT * j + CT],
                                           start=(j == 0), stop=(j == KS - 1))
                ins.then_inc(s_proj, 1)

            def back(c):
                pe.wait_ge(s_oT, c + 1)
                if valid(c + 3):
                    pe.wait_ge(s_qkv, 3 * (c + 3) + 2)
                else:
                    pe.wait_ge(s_res, c)
                wait(pe, s_g, GS * (c - 2) + 1)
                for t in range(TPC):
                    ins = nc.tensor.transpose(bank[0][0:TT, C * t:C * t + C], oT[:, TT * t:TT * t + TT], ident[:, :])
                ins.then_inc(s_oback, 1)

            def gate_transposes(g, par):
                pe.wait_ge(s_xrow, g + 1)
                pe.wait_ge(s_res, min(g + 2, NC) if isinstance(g, int) else g + 2)
                for t in range(TPC):
                    ins = nc.tensor.transpose(bank[0][:, TT * t:TT * t + TT], xrow[par][:, t, 0:C], ident[0:TT, 0:TT])
                ins.then_inc(s_gT, 1)

            def gate_logits(g):
                pe.wait_ge(s_gxT, g + 1)
                for t in range(TPC):
                    ins = nc.tensor.matmul(bank[0][0:TT, NE * t:NE * t + NE], gxT[:, TT * t:TT * t + TT], wg_sb[:, :],
                                           start=True, stop=True)
                ins.then_inc(s_lg, 1)

            def ranks(g):
                pe.wait_ge(s_g, GS * g + GS)
                wait(pe, s_slot, SLS * g)
                pe.wait_ge(s_sc, SMS * min(g + 3, NC - 1) + 1 if isinstance(g, int) else SMS * (g + 3) + 1)
                r = bank[3][0:TT, RANKS:RANKS + TPC * NE].rearrange("p (t e) -> p t e", t=TPC)
                nc.tensor.matmul(r, before[:, :], chosen[:, :, :], start=True, stop=False)
                for t in range(1, TPC):
                    nc.tensor.matmul(r[:, t:TPC, :], ones16[:, :], chosen[:, 0:TPC - t, :], start=False, stop=False)
                nc.tensor.matmul(r, ones16[:, :], view(counted, TT, 0, [0, TPC], [1, NE]), start=False, stop=True
                                 ).then_inc(s_rank, 1)

            def attention(c, par, inside):
                if inside(2):
                    transposes(c + 2, par)
                if inside(0):
                    spread(c)
                if inside(-3):
                    ranks(c - 3)
                if inside(2):
                    qkv(c + 2, par)
                if inside(-1):
                    back(c - 1)
                if inside(1):
                    scores(c + 1, 1 - par)
                if inside(-2):
                    gate_transposes(c - 2, par)
                if inside(1):
                    scores_rest(c + 1, 1 - par)
                if inside(-2):
                    gate_logits(c - 2)
                if inside(0):
                    project(c)

            pe.wait_ge(s_const, 8)
            over_chunks(nc.tensor, attention)

            pe.wait_ge(s_slot, SLS * NC)
            nc.tensor.matmul(bank[3][0:TT, 0:NE], ones16[:, :], counted[:, :], start=True, stop=True
                             ).then_inc(s_total, 1)

            pe.wait_ge(s_whalves, 32)
            pe.wait_ge(s_table, TABLE)

            def block_transposes(b, buf):
                pe.wait_ge(s_xb[buf], 4 * (b - buf) + 16)
                wait(pe, s_xl, b)
                for t in range(SPT):
                    ins = nc.tensor.transpose(bank[4][:, 128 * t:128 * t + 128], xb[buf][:, t, 0:C], ident[:, :])
                ins.then_inc(s_xbT, 1)

            def inner(b, par, e):
                pe.wait_ge(s_xl, b + 1)
                for i in range(FC):
                    wait(pe, s_gelu, FC * (b - 1) + i + 1)
                    off = e * FF + C * i
                    dst = bank[i][:, 0:BLK]
                    nc.tensor.matmul(dst, w1_hi[:, bass.ds(off, C)], xh[par][:, :], start=True, stop=False)
                    nc.tensor.matmul(dst, w1_hi[:, bass.ds(off, C)], xl[par][:, :], start=False, stop=False)
                    nc.tensor.matmul(dst, w1_lo[:, bass.ds(off, C)], xh[par][:, :], start=False, stop=True
                                     ).then_inc(s_h, 1)

            def outer(b, par, e):
                pe.wait_ge(s_split, FC * b + FC)
                wait(pe, s_ev, b - 1)
                for t in range(SPT):
                    for i in range(FC):
                        off = e * FF + C * i
                        a = BLK * i + 128 * t
                        dst = bank[5 + par][:, 128 * t:128 * t + 128]
                        nc.tensor.matmul(dst, act_hi[par][:, a:a + 128], w2_hi[:, bass.ds(off, C)],
                                         start=(i == 0), stop=False)
                        nc.tensor.matmul(dst, act_hi[par][:, a:a + 128], w2_lo[:, bass.ds(off, C)],
                                         start=False, stop=False)
                        ins = nc.tensor.matmul(dst, act_lo[par][:, a:a + 128], w2_hi[:, bass.ds(off, C)],
                                               start=False, stop=(i == FC - 1))
                ins.then_inc(s_y, 1)

            def expert_of(b):
                return nc.tensor.value_load(tab_e[0:1, bass.ds(b, 1)], min_val=0, max_val=NE - 1)

            def experts(b, u, inside):
                if inside(1):
                    block_transposes(b + 1, (u + 1) % 4)
                if inside(0):
                    inner(b, u % 2, expert_of(b))
                if inside(-1):
                    outer(b - 1, (u - 1) % 2, expert_of(b - 1))

            over_blocks(nc.tensor, experts)

        @block.scalar
        def _(act):
            act.wait_ge(s_wT, 1)
            nc.scalar.copy(w_tap[:, 0:2, :].rearrange("p a o -> p (a o)"), bank[7][:, 0:256])
            nc.scalar.copy(w_tap[0:64, 2, :], bank[7][0:64, 256:384]).then_inc(s_wtap, 1)

            def keep_frames(c, par):
                act.wait_ge(s_xTp, c + 1)
                wait(act, s_conv, c - 1)
                nc.scalar.copy(xT[par][:, :], bank[par][:, :]).then_inc(s_xT, 1)

            def relu(c, par):
                act.wait_ge(s_conv, c + 1)
                nc.scalar.activation(chan_cols(c), bank[2 + par][:, 0:CT], ACT.Relu, bias=tok_b_c
                                     ).then_inc(s_relu, 1)

            act.wait_ge(s_cols, 1)
            nc.scalar.copy(cols[:, 0:7 + NE * FC], bank[6][:, 0:7 + NE * FC]).then_inc(s_cols, 1)
            act.wait_ge(s_cols, 2)
            keep_frames(0, 0)
            for c in range(1, 4):
                keep_frames(c, c % 2)
                relu(c - 1, (c - 1) % 2)
            with nc.scalar.Fori(1, NC // 4) as p:
                for u in range(4):
                    c = 4 * p + u
                    keep_frames(c, u % 2)
                    relu(c - 1, (u - 1) % 2)
            relu(NC - 1, (NC - 1) % 2)

            act.wait_ge(s_bn, 2)
            nc.scalar.activation(bn_w[:, 1:2], bn_w[:, 0:1], ACT.Sqrt).then_inc(s_bnsq, 1)

            def keep_tiles(c, par):
                act.wait_ge(s_zT, c + 1)
                nc.scalar.copy(tile_rows(tokens, c), bank[par][0:TT, :].rearrange("p (t c) -> p t c", t=TPC)
                               ).then_inc(s_tok, 1)

            pairs(nc.scalar, keep_tiles)

            act.wait_ge(s_ln, LN_STEPS)
            nc.scalar.activation(ln_c[:, :], ln_b[:, :], ACT.Sqrt).then_inc(s_lnsq, 1)

            def normalise(c, par, signal):
                for t in range(TPC):
                    i = c * TPC + t
                    ins = nc.scalar.activation(xn[par][:, t, :], view_tile(i), ACT.Identity,
                                               bias=nmr[:, bass.ds(i, 1)], scale=rstd[:, bass.ds(i, 1)])
                ins.then_inc(signal, 1)

            def view_tile(i):
                return tokens[:, bass.ds(i, 1), :].rearrange("p a c -> p (a c)")

            def attention(c, par, inside):
                if inside(-1):
                    act.wait_ge(s_proj, c)
                    wait(act, s_oback, c - 1)
                    nc.scalar.activation(oT[:, :], bank[1][:, 0:CT], ACT.Identity, bias=proj_b_c,
                                         scale=1.0 / PSCALE).then_inc(s_oT, 1)
                if inside(2):
                    act.wait_ge(s_xnTp, c + 3)
                    wait(act, s_qkvp, 3 * (c + 1))
                    nc.scalar.copy(xnT[par][:, :], bank[0][:, 0:CT]).then_inc(s_xnT, 1)
                    for i, (dst, b) in enumerate(((q, 1), (k, 0), (v, 1))):
                        act.wait_ge(s_qkvp, 3 * (c + 2) + i + 1)
                        if i == 0:
                            wait(act, s_qk, c + 1)
                        if i == 2:
                            wait(act, s_pv, NG * (c + 1))
                        nc.scalar.activation(dst[par][:, :], bank[b][:, 0:CT], ACT.Identity,
                                             bias=qb_c if i == 0 else qkv_b_c[:, i:i + 1],
                                             scale=QSCALE if i == 0 else 1.0).then_inc(s_qkv, 1)
                if inside(-2):
                    g = c - 2
                    act.wait_ge(s_gln, GLN * g + GLN)
                    wait(act, s_scat, ROUTES * (g - 1))
                    for t in range(TPC):
                        ins = nc.scalar.activation(xrow[par][:, t, 0:C], view_tile(g * TPC + t), ACT.Identity,
                                                   bias=gnmr[par][:, t:t + 1], scale=grstd[par][:, t:t + 1])
                    ins.then_inc(s_xrow, 1)
                if inside(3):
                    wait(act, s_xnTp, c + 2)
                    normalise(c + 3, 1 - par, s_xn)
                if inside(-2):
                    act.wait_ge(s_gT, c - 1)
                    wait(act, s_lg, c - 2)
                    nc.scalar.copy(gxT[:, :], bank[0][:, 0:CT]).then_inc(s_gxT, 1)
                if inside(1):
                    act.wait_ge(s_sc, SMS * (c + 1) + 3)
                    nc.scalar.activation(ex[:, :, :], sc[:, :, :], ACT.Exp).then_inc(s_exp, 1)
                if inside(-2):
                    act.wait_ge(s_g, GS * (c - 2) + 3)
                    nc.scalar.activation(pr[:, :, :], lg[:, :, :], ACT.Exp).then_inc(s_gexp, 1)
                if inside(1):
                    act.wait_ge(s_sc, SMS * (c + 1) + 6)
                    wait(act, s_px, NG * (c + 1))
                    nc.scalar.copy(p_hi[:, :, :], sc[:, :, :]).then_inc(s_hi, 1)

            act.wait_ge(s_ln, LN_STEPS + 2)
            act.wait_ge(s_tok, NC)
            over_chunks(nc.scalar, attention)

            act.wait_ge(s_table, TABLE)
            act.wait_ge(s_scat, ROUTES * NC)
            act.wait_ge(s_pads, 16 * (NE + 1))

            def experts(b, u, inside):
                if inside(3):
                    buf = (u + 3) % 4
                    wait(act, s_xbT, b)
                    wait(act, s_ids, b)
                    row = nc.scalar.value_load(tab_row[0:1, bass.ds(b + 3, 1)], min_val=0, max_val=NE * REGION)
                    act.dma_start(xb[buf][:, :, :], slots[bass.ds(row, BLK), :].rearrange("(k p) c -> p k c", p=128)
                                  ).then_inc(s_xb[buf], 16)
                if inside(1):
                    act.wait_ge(s_xbT, b + 2)
                    wait(act, s_h, FC * b)
                    nc.scalar.activation(xh[(u + 1) % 2][:, :], bank[4][:, 0:BLK], ACT.Copy, scale=XSCALE
                                         ).then_inc(s_xh, 1)
                if inside(0):
                    e = nc.scalar.value_load(tab_e[0:1, bass.ds(b, 1)], min_val=0, max_val=NE - 1)
                    wait(act, s_split, FC * (b - 1))
                    for i in range(FC):
                        act.wait_ge(s_h, FC * b + i + 1)
                        nc.scalar.activation(act32[u % 2][:, BLK * i:BLK * i + BLK], bank[i][:, 0:BLK],
                                             ACT.Gelu_apprx_tanh, bias=b1_c[:, bass.ds(e * FC + i, 1)],
                                             scale=1.0 / (XSCALE * WSCALE)).then_inc(s_gelu, 1)

            over_blocks(nc.scalar, experts)

        @block.vector
        def _(dve):
            V = nc.vector
            dve.wait_ge(s_bias, 16 * N_BIAS)
            dve.wait_ge(s_par, 16 * N_PAR)
            dve.wait_ge(s_cols, 2)
            V.tensor_copy(bias[:, :, :], view(rel_bias, 128, HALF, [1, KS], [0, SUB])).then_inc(s_bn, 1)
            V.tensor_scalar(qb_c, cols[:, 4:5], QSCALE, None, ALU.mult)
            dve.wait_ge(s_bn, 1)
            for n in range(HALF):
                V.tensor_copy(bias[0:32, :, n], rel_bias[0:32, KS - 1 - n:2 * KS - 1 - n])
                V.tensor_copy(bias[32:64, :, SUB - HALF + n], rel_bias[32:64, HALF - 1 - n:HALF - 1 - n + KS])

            def stats(c):
                dve.wait_ge(s_relu, c + 1)
                V.bn_stats(bn_st[:, bass.ds(c, 1), :].rearrange("p a s -> p (a s)"), chan_cols(c)).then_inc(s_bnst, 1)

            stats(0)
            with V.Fori(1, NC - 1) as c:
                stats(c)
            stats(NC - 1)
            dve.wait_ge(s_bnst, NC)
            V.bn_aggr(bn_mv[:, :], bn_st[:, :, :].rearrange("p a s -> p (a s)")).then_inc(s_bnst, 1)
            dve.wait_ge(s_bnst, NC + 1)
            V.tensor_scalar(bn_w[:, 0:1], bn_mv[:, 1:2], EPS, None, ALU.add).then_inc(s_bn, 1)
            dve.wait_ge(s_bnsq, 1)
            V.reciprocal(bn_w[:, 2:3], bn_w[:, 1:2]).then_inc(s_bn, 1)
            dve.wait_ge(s_bn, 3)
            V.tensor_tensor(bn_w[:, 3:4], bn_w[:, 2:3], gamma_c, ALU.mult).then_inc(s_bn, 1)
            dve.wait_ge(s_bn, 4)
            V.tensor_tensor(bn_mv[:, 1:2], bn_mv[:, 0:1], bn_w[:, 3:4], ALU.mult).then_inc(s_bn, 1)
            dve.wait_ge(s_bn, 5)
            V.tensor_tensor(bn_w[:, 0:1], beta_c, bn_mv[:, 1:2], ALU.subtract).then_inc(s_bn, 1)
            dve.wait_ge(s_bn, 6)

            def affine(c, par):
                wait(dve, s_zT, c - 1)
                V.tensor_scalar(zc[par][:, :], chan_cols(c), bn_w[:, 3:4], bn_w[:, 0:1], ALU.mult, ALU.add
                                ).then_inc(s_zc, 1)

            def tile_stats(c):
                for t in range(TPC):
                    i = c * TPC + t
                    ins = V.bn_stats(ln_stats[:, bass.ds(i, 1), :].rearrange("p a s -> p (a s)"),
                                     tokens[:, bass.ds(i, 1), :].rearrange("p a c -> p (a c)"))
                return ins

            def normalise_channels(c, par):
                affine(c, par)
                if not isinstance(c, int) or c > 0:
                    dve.wait_ge(s_tok, c)
                    tile_stats(c - 1).then_inc(s_lnst, 1)

            pairs(V, normalise_channels)
            dve.wait_ge(s_tok, NC)
            tile_stats(NC - 1).then_inc(s_lnst, 1)

            def layer_norm():
                n = [0]

                def step(ins):
                    n[0] += 1
                    ins.then_inc(s_ln, 1)
                    dve.wait_ge(s_ln, n[0])
                me, ve, mo, vo = (ln_stats[:, :, i] for i in (1, 2, 4, 5))
                step(V.tensor_tensor(ln_a[:, :], me, mo, ALU.subtract))
                step(V.tensor_tensor(ln_b[:, :], ve, vo, ALU.add))
                step(V.tensor_tensor(ln_c[:, :], me, mo, ALU.add))
                step(V.tensor_tensor(ln_a[:, :], ln_a[:, :], ln_a[:, :], ALU.mult))
                step(V.tensor_scalar(ln_b[:, :], ln_b[:, :], 1.0 / C, EPS, ALU.mult, ALU.add))
                step(V.scalar_tensor_tensor(ln_b[:, :], ln_a[:, :], 0.25, ln_b[:, :], ALU.mult, ALU.add))
                step(V.tensor_scalar(ln_a[:, :], ln_c[:, :], -0.5, None, ALU.mult))
                dve.wait_ge(s_lnsq, 1)
                step(V.reciprocal(rstd[:, :], ln_c[:, :]))
                step(V.tensor_tensor(nmr[:, :], ln_a[:, :], rstd[:, :], ALU.mult))

            dve.wait_ge(s_lnst, NC)
            layer_norm()

            def products(c, par):
                dve.wait_ge(s_qkv, 3 * c + 2)
                wait(dve, s_score, c - 1)
                for b in range(CB):
                    o = L * b
                    V.tensor_tensor(view(qk[par], C, o + HALF, [CT, KS], [1, L - 2 * HALF]),
                                    view(q[par], C, o + HALF, [0, KS], [1, L - 2 * HALF]),
                                    view(k[par], C, o, [1, KS], [1, L - 2 * HALF]), ALU.mult)
                    for t0, k0 in ((o, o), (o + L - HALF, o + L - KS)):
                        ins = V.tensor_tensor(view(qk[par], C, t0, [CT, KS], [1, HALF]),
                                              view(q[par], C, t0, [0, KS], [1, HALF]),
                                              view(k[par], C, k0, [1, KS], [0, HALF]), ALU.mult)
                ins.then_inc(s_qk, 1)

            def softmax(c):
                def step(ins, i):
                    ins.then_inc(s_sc, 1)
                    dve.wait_ge(s_sc, SMS * c + i)
                by_token = [1, SUB], [SUB, KS]
                rows = sc[:, :, :].rearrange("p j n -> p (j n)")
                bias_rows = bias[:, :, :].rearrange("p j n -> p (j n)")
                dve.wait_ge(s_score, c + 1)
                wait(dve, s_hi, c)
                V.tensor_tensor(rows[:, 0:JA * SUB], bank[2][:, 0:JA * SUB], bias_rows[:, 0:JA * SUB], ALU.add)
                step(V.tensor_tensor(rows[:, JA * SUB:], bank[3][:, 0:JB * SUB], bias_rows[:, JA * SUB:], ALU.add), 1)
                step(V.tensor_reduce(mx[:, :], view(sc, 128, 0, *by_token), AX.X, ALU.max), 2)
                step(V.tensor_tensor(sc[:, :, :], sc[:, :, :], view(mx, 128, 0, [0, KS], [1, SUB]), ALU.subtract), 3)

            def softmax_rest(c):
                def step(ins, i):
                    ins.then_inc(s_sc, 1)
                    dve.wait_ge(s_sc, SMS * c + i)
                by_token = [1, SUB], [SUB, KS]
                dve.wait_ge(s_exp, c + 1)
                step(V.tensor_reduce(sm[:, :], view(ex, 128, 0, *by_token), AX.X, ALU.add), 4)
                step(V.reciprocal(rs[:, :], sm[:, :]), 5)
                step(V.scalar_tensor_tensor(sc[:, :, :], ex[:, :, :], PSCALE, view(rs, 128, 0, [0, KS], [1, SUB]),
                                            ALU.mult, ALU.mult), 6)
                dve.wait_ge(s_hi, c + 1)
                V.tensor_tensor(p_lo[:, :, :], sc[:, :, :], p_hi[:, :, :], ALU.subtract).then_inc(s_sc, 1)

            def weigh(c, par):
                wait(dve, s_proj, c)
                for g in range(NG):
                    dve.wait_ge(s_px, NG * c + g + 1)
                    s = g % SPB
                    o = SUB * g
                    lo = HALF if s == 0 else 0
                    hi = SUB - HALF if s == SPB - 1 else SUB
                    start = L * (g // SPB)
                    for j0, nj, b in ((0, JA, 4), (JA, JB, 5)):
                        b += 2 * (g % 2)
                        parts = [(lo, hi - lo, o + lo - HALF, 1)]
                        if s == 0:
                            parts.append((0, HALF, start, 0))
                        if s == SPB - 1:
                            parts.append((hi, HALF, start + L - KS, 0))
                        for n0, nn, v0, step in parts:
                            ins = V.tensor_tensor(view(pv, C, CT * j0 + o + n0, [CT, nj], [1, nn]),
                                                  view(bank[b], C, n0, [SUB, nj], [1, nn]),
                                                  view(v[par], C, v0 + j0, [1, nj], [step, nn]), ALU.mult)
                    ins.then_inc(s_pv, 1)

            def residual(c, par):
                dve.wait_ge(s_oback, c + 1)
                V.tensor_tensor(tile_rows(tokens, c), bank[0][0:TT, :].rearrange("p (t c) -> p t c", t=TPC),
                                tile_rows(tokens, c), ALU.add).then_inc(s_res, 1)
                dve.wait_ge(s_res, c + 1)
                wait_alone(dve, s_gln, GLN * (c - 1))
                for t in range(TPC):
                    row = tokens[:, bass.ds(c * TPC + t, 1), :].rearrange("p a c -> p (a c)")
                    ins = V.bn_stats(gst[par][:, t, :], row)
                ins.then_inc(s_gstat, 1)

            def small(counter, per, g, ins, i):
                ins.then_inc(counter, 1)
                dve.wait_ge(counter, per * g + i)

            def gate_read(g):
                dve.wait_ge(s_lg, g + 1)
                small(s_g, GS, g, V.tensor_tensor(lg[:, :, :],
                                                  bank[0][0:TT, 0:TPC * NE].rearrange("p (t e) -> p t e", t=TPC),
                                                  view(bg_sb, TT, 0, [0, TPC], [1, NE]), ALU.add), 1)
                small(s_g, GS, g, V.tensor_reduce(gm[:, :], lg[:, :, :], AX.X, ALU.max), 2)
                small(s_g, GS, g, V.tensor_tensor(lg[:, :, :], lg[:, :, :], per_tile(gm), ALU.subtract), 3)

            def per_tile(t):
                return view(t, TT, 0, [1, TPC], [0, NE])

            def gate_choose(g):
                def step(ins, i):
                    small(s_g, GS, g, ins, i)
                rank = view(expert_rank, TT, 0, [0, TPC], [1, NE])
                dve.wait_ge(s_gexp, g + 1)
                wait(dve, s_weight, g)
                step(V.tensor_reduce(gs[:, :], pr[:, :, :], AX.X, ALU.add), 4)
                step(V.reciprocal(gm[:, :], gs[:, :]), 5)
                step(V.tensor_tensor(pr[:, :, :], pr[:, :, :], per_tile(gm), ALU.mult), 6)
                n = 6
                for j, values in enumerate((pr, lg)):
                    h = hot[:, j, :, :]
                    step(V.tensor_reduce(top[:, j, :], values[:, :, :], AX.X, ALU.max), n + 1)
                    step(V.tensor_tensor(h, values[:, :, :], view(top, TT, TPC * j, [1, TPC], [0, NE]), ALU.is_equal), n + 2)
                    step(V.tensor_tensor(h, h, rank, ALU.mult), n + 3)
                    step(V.tensor_reduce(gs[:, :], h, AX.X, ALU.max), n + 4)
                    if j == 0:
                        step(V.tensor_tensor(h, rank, per_tile(gs), ALU.is_equal), n + 5)
                        V.scalar_tensor_tensor(lg[:, :, :], h, -2.0, pr[:, :, :], ALU.mult, ALU.add).then_inc(s_pr, 1)
                        dve.wait_ge(s_pr, g + 1)
                    else:
                        V.tensor_tensor(h, rank, per_tile(gs), ALU.is_equal).then_inc(s_hot, 1)
                        dve.wait_ge(s_hot, g + 1)
                    n += 5
                step(V.tensor_tensor(chosen[:, :, :], hot[:, 0, :, :], hot[:, 1, :, :], ALU.add), 16)

            def gate_slots(g, par):
                dve.wait_ge(s_rank, g + 1)
                small(s_slot, SLS, g, V.tensor_tensor(
                    slot[:, :, :], bank[3][0:TT, RANKS:RANKS + TPC * NE].rearrange("p (t e) -> p t e", t=TPC),
                    view(region, TT, 0, [0, TPC], [1, NE]), ALU.add), 1)
                small(s_slot, SLS, g, V.tensor_tensor(
                    hit[:, :, :, :].rearrange("p j t e -> p j (t e)"), hot[:, :, :, :].rearrange("p j t e -> p j (t e)"),
                    view(slot, TT, 0, [0, TOP], [1, TPC * NE]), ALU.mult), 2)
                small(s_slot, SLS, g, V.tensor_reduce(
                    pos[:, :, :].rearrange("p j t -> p (j t)"), hit[:, :, :, :].rearrange("p j t e -> p (j t) e"),
                    AX.X, ALU.add), 3)
                wait(dve, s_scat, ROUTES * (g - 1))
                small(s_slot, SLS, g, V.tensor_copy(idx[par][:, :, :], pos[:, :, :]), 4)
                with nc.allow_low_precision(reason="counts up to 256 are exact in float16"):
                    small(s_slot, SLS, g, V.tensor_reduce(fresh[:, :], view(chosen, TT, 0, [1, NE], [NE, TPC]),
                                                          AX.X, ALU.add), 5)
                small(s_slot, SLS, g, V.tensor_tensor(counted[:, :], counted[:, :], fresh[:, :], ALU.add), 6)

            def attention(c, par, inside):
                if inside(0):
                    weigh(c, par)
                if inside(-3):
                    gate_slots(c - 3, 1 - par)
                if inside(-1):
                    residual(c - 1, 1 - par)
                if inside(2):
                    products(c + 2, par)
                if inside(1):
                    softmax(c + 1)
                if inside(-2):
                    gate_read(c - 2)
                if inside(1):
                    softmax_rest(c + 1)
                if inside(-2):
                    gate_choose(c - 2)

            dve.wait_ge(s_gconst, N_GCONST)
            over_chunks(V, attention)

            n = [0]

            def step(ins):
                n[0] += 1
                ins.then_inc(s_table, 1)
                dve.wait_ge(s_table, n[0])

            dve.wait_ge(s_total, 1)
            step(V.tensor_copy(tb_n[:, :], bank[3][0:TT, 0:NE]))
            step(V.tensor_tensor(tb_k[:, :, :], view(tb_n, 1, 0, [1, NE], [0, MAXB]), tb_thr[:, :, :], ALU.is_gt))
            step(V.tensor_reduce(tb_blocks[:, :], tb_k[:, :, :], AX.X, ALU.add))
            step(V.tensor_tensor(tb_tmp[:, :, :], view(tb_blocks, 1, 0, [0, NE], [1, NE]), tb_tri[:, :, :], ALU.mult))
            step(V.tensor_reduce(tb_ends[:, :], tb_tmp[:, :, :], AX.X, ALU.add))
            step(V.tensor_tensor(tb_past[:, :, :], view(tb_id, 1, 0, [1, NB], [0, NE]),
                                 view(tb_ends, 1, 0, [0, NB], [1, NE]), ALU.is_ge))
            step(V.tensor_reduce(tb_e[:, :], tb_past[:, :, :], AX.X, ALU.add))
            step(V.tensor_tensor(tb_past[:, :, :], tb_past[:, :, :], view(tb_blocks, 1, 0, [0, NB], [1, NE]), ALU.mult))
            step(V.tensor_reduce(tb_s[:, :], tb_past[:, :, :], AX.X, ALU.add))
            step(V.tensor_tensor(tb_s[:, :], tb_id[:, :], tb_s[:, :], ALU.subtract))
            step(V.tensor_scalar(tb_u[:, :], tb_e[:, :], float(NE), float(BLK), ALU.is_lt, ALU.mult))
            step(V.tensor_tensor(tb_s[:, :], tb_s[:, :], tb_u[:, :], ALU.mult))
            step(V.tensor_scalar(tab_e[:, :], tb_e[:, :], float(NE - 1), None, ALU.min))
            step(V.scalar_tensor_tensor(tab_row[:, :], tb_e[:, :], float(REGION), tb_s[:, :], ALU.mult, ALU.add))
            step(V.tensor_tensor(tab_pad[:, :], tb_n[0:1, :], region[0:1, :], ALU.add))
            assert n[0] == TABLE

            def experts(b, u, inside):
                if inside(1):
                    par = (u + 1) % 2
                    dve.wait_ge(s_xh, b + 2)
                    V.scalar_tensor_tensor(xl[par][:, :], bank[4][:, 0:BLK], XSCALE, xh[par][:, :], ALU.mult,
                                           ALU.subtract).then_inc(s_xl, 1)
                    wait(dve, s_ysc[par], sent(b - 3, par))
                    V.tensor_copy(ids[(u + 1) % 4][:, :], xb[(u + 1) % 4][:, :, C:C + 1].bitcast(I32).rearrange(
                        "p k a -> p (k a)")).then_inc(s_ids, 1)
                if inside(0):
                    par = u % 2
                    wait(dve, s_y, b - 1)
                    for i in range(FC):
                        part = slice(BLK * i, BLK * i + BLK)
                        dve.wait_ge(s_gelu, FC * b + i + 1)
                        V.tensor_scalar(act_hi[par][:, part], act32[par][:, part], HSCALE, None, ALU.mult
                                        ).then_inc(s_hi32, 1)
                        dve.wait_ge(s_hi32, FC * b + i + 1)
                        V.scalar_tensor_tensor(act_lo[par][:, part], act32[par][:, part], HSCALE, act_hi[par][:, part],
                                               ALU.mult, ALU.subtract).then_inc(s_split, 1)
                if inside(-1):
                    par = (u - 1) % 2
                    e = nc.vector.value_load(tab_e[0:1, bass.ds(b - 1, 1)], min_val=0, max_val=NE - 1)
                    dve.wait_ge(s_y, b)
                    wait(dve, s_ysc[par], sent(b - 3, par))
                    for k in range(SPT):
                        ins = V.scalar_tensor_tensor(
                            ys[par][:, k, :], bank[5 + par][:, 128 * k:128 * k + 128], 1.0 / (HSCALE * WSCALE),
                            b2_sb[:, bass.ds(e, 1), :].rearrange("p a c -> p (a c)"), ALU.mult, ALU.add)
                    ins.then_inc(s_ev, 1)

            over_blocks(V, experts)

            def combine(c, u):
                for j in range(TOP):
                    for t in range(TPC):
                        i = c * TPC + t
                        row = tokens[:, bass.ds(i, 1), :].rearrange("p a c -> p (a c)")
                        ins = V.scalar_tensor_tensor(row, comb[u][:, j, C * t:C * t + C],
                                                     weight[:, j, bass.ds(i, 1)], row, ALU.mult, ALU.add)
                    if j == 0:
                        ins.then_inc(s_first, 1)
                        dve.wait_ge(s_first, c + 1)
                ins.then_inc(s_acc, 1)

            with V.Fori(0, NC // 4) as p:
                for u in range(4):
                    dve.wait_ge(s_comb[u], 32 * p + 32)
                    combine(4 * p + u, u)


_INS = ["x", "L0_tok_W", "L0_tok_b", "L0_tok_gamma", "L0_tok_beta", "L0_attn_qkv_w", "L0_attn_qkv_b",
        "L0_attn_rpb", "L0_attn_proj_w", "L0_attn_proj_b", "L0_ffn_Wg", "L0_ffn_bg", "L0_ffn_W1", "L0_ffn_b1",
        "L0_ffn_W2", "L0_ffn_b2"]


def kernel(**inputs):
    import numpy as _np
    import concourse.bacc as _bacc
    from concourse import mybir as _mybir
    from concourse.bass_utils import run_bass_kernel_spmd as _run

    nc = _bacc.Bacc("TRN2", target_bir_lowering=False, num_devices=1)
    arrays, args = {}, []
    for name in _INS:
        a = _np.ascontiguousarray(inputs[name])
        arrays[f"in_{name}_dram"] = a
        args.append(nc.dram_tensor(f"in_{name}_dram", a.shape, _mybir.dt.from_np(a.dtype), kind="ExternalInput").ap())
    out = nc.dram_tensor("out_dram", (B, L, C), F32, kind="ExternalOutput").ap()
    tower(nc, *args, out)
    r = _run(nc, [arrays], core_ids=[0])
    return r.results[0]["out_dram"]
```
